# Optimizing a Trainium2 kernel written in Bass

```python
import numpy as np
import jax
import jax.numpy as jnp

def _softmax(x, axis=-1):
    return jax.nn.softmax(x, axis=axis)

def _gelu(x):
    return jax.nn.gelu(x, approximate=True)

def _silu(x):
    return jax.nn.silu(x)

def _sigmoid(x):
    return jax.nn.sigmoid(x)

def _layernorm(x, axis=-1, eps=1e-05):
    m = jnp.mean(x, axis=axis, keepdims=True)
    v = jnp.var(x, axis=axis, keepdims=True)
    return (x - m) / jnp.sqrt(v + eps)

def _scatter_add(tgt, idx, src, axis=0):
    return tgt.at[idx].add(src)

def _segment_sum(src, seg, n):
    return jax.ops.segment_sum(src, seg, n)
kernel_name = 'mk_perceiver_d1_seqx_r8_647c93'

def setup_inputs(seed: int=0):
    np.random.seed(seed)
    _w = jnp.asarray

    def _rec_inputs():
        import jax
        import jax.numpy as jnp
        _rk = jax.random.key(seed)
        x = -0.0003929 + 0.9999 * jax.random.normal(jax.random.fold_in(_rk, 1), (16, 32, 128), jnp.float32)
        _lenS = 32 - jax.random.randint(jax.random.fold_in(_rk, 7), (16,), 0, max(1, 32 // 4) + 1, jnp.int32)
        _lenS2 = 512 - jax.random.randint(jax.random.fold_in(_rk, 8), (16,), 0, max(1, 512 // 4) + 1, jnp.int32)
        _ctx_1024P = jax.random.normal(jax.random.fold_in(_rk, 11), (16, 16, 128), jnp.float32)
        _ctx_1024c = jax.random.dirichlet(jax.random.fold_in(_rk, 511), 0.3 * jnp.ones((16,), jnp.float32), (16, 512))
        _ctx_1024t = jnp.einsum('bsk,bkd->bsd', _ctx_1024c, _ctx_1024P)
        _ctx_1024t = _ctx_1024t * jax.lax.rsqrt(jnp.mean(jnp.square(_ctx_1024t)) + 1e-12) * 0.953939
        ctx_1024 = -3.05549e-07 + 0.0199987 * (_ctx_1024t + 0.3 * jax.random.normal(jax.random.fold_in(_rk, 611), (16, 512, 128), jnp.float32))
        return (x, ctx_1024)
    x, ctx_1024 = _rec_inputs()

    def _L0_xattn_setup():
        import jax, jax.numpy as jnp
        import numpy as np
        E, T, H, F = (8, 256, 128, 512)
        key = jax.random.key(seed)
        k1, k2, k3 = jax.random.split(key, 3)
        x = jax.random.normal(k1, (E, T, H), dtype=jnp.float32)
        w1 = jax.random.normal(k2, (E, F, H), dtype=jnp.float32) * 0.02
        w2 = jax.random.normal(k3, (E, F, H), dtype=jnp.float32) * 0.02
        return {'x': x, 'w1': w1, 'w2': w2}
    _L0_xattn_all = _L0_xattn_setup()
    _L0_xattn_in = {k: v for k, v in _L0_xattn_all.items() if k in ()}
    del _L0_xattn_all

    def _L0_attn_setup():
        import jax, jax.numpy as jnp
        import numpy as np
        import math
        D = 128
        H = 16
        HD = D // H
        NKV = H // 4
        SPARSE_K = 64
        TEMP = 1.0
        EPS = 1e-08

        def rmsnorm(x, w):
            return x * jax.lax.rsqrt(jnp.mean(x * x, axis=-1, keepdims=True) + EPS) * w

        def alibi_bias(n_head, T):
            slopes = 2.0 ** (-(jnp.arange(n_head, dtype=jnp.float32) / (n_head - 1) * 8.0))
            pos = jnp.arange(T)
            dist = jnp.abs(pos[:, None] - pos[None, :]).astype(jnp.float32)
            return -slopes[:, None, None] * dist[None, :, :]
        key = jax.random.key(seed)
        ks = jax.random.split(key, 8)
        B, T = (1, 256)
        s = 0.02
        return {'x': jax.random.normal(ks[0], (B, T, D), dtype=jnp.float32), 'wq': jax.random.normal(ks[1], (D, H * HD), dtype=jnp.float32) * s, 'bq': jnp.zeros((H * HD,), dtype=jnp.float32), 'wkv': jax.random.normal(ks[2], (D, 2 * NKV * HD), dtype=jnp.float32) * s, 'bkv': jnp.zeros((2 * NKV * HD,), dtype=jnp.float32), 'wo': jax.random.normal(ks[3], (H * HD, D), dtype=jnp.float32) * s, 'bo': jnp.zeros((D,), dtype=jnp.float32), 'qn_w': jnp.ones((HD,), dtype=jnp.float32), 'kn_w': jnp.ones((HD,), dtype=jnp.float32)}
    _L0_attn_all = _L0_attn_setup()
    _L0_attn_in = {k: v for k, v in _L0_attn_all.items() if k in ('wq', 'bq', 'wkv', 'bkv', 'wo', 'bo', 'qn_w', 'kn_w')}
    del _L0_attn_all

    def _L0_ffn_setup():
        import jax, jax.numpy as jnp
        import numpy as np
        E, K = (8, 2)
        DM, DE = (128, 352)
        B, S = (1, 256)
        EPS = 1e-06

        def _rmsnorm(x, w):
            var = jnp.mean(jnp.square(x), axis=-1, keepdims=True)
            return x * jax.lax.rsqrt(var + EPS) * w
        key = jax.random.key(seed)
        kx, kg, k1, k2, k3 = jax.random.split(key, 5)

        def kaiming_uniform(k, shape, fan_in):
            bound = 1.0 / np.sqrt(fan_in)
            return jax.random.uniform(k, shape, jnp.float32, -bound, bound)
        return {'x': jax.random.normal(kx, (B, S, DM), jnp.float32), 'gate_w': kaiming_uniform(kg, (E, DM), DM), 'rms_w': jnp.ones((DM,), jnp.float32), 'W1': kaiming_uniform(k1, (E, DE, DM), DE * DM), 'W2': kaiming_uniform(k2, (E, DE, DM), DE * DM), 'W3': kaiming_uniform(k3, (E, DM, DE), DM * DE)}
    _L0_ffn_all = _L0_ffn_setup()
    _L0_ffn_in = {k: v for k, v in _L0_ffn_all.items() if k in ('gate_w', 'rms_w', 'W1', 'W2', 'W3')}
    del _L0_ffn_all
    return {'x': x, 'ctx_1024': ctx_1024, 'L0_attn_wq': _L0_attn_in['wq'], 'L0_attn_bq': _L0_attn_in['bq'], 'L0_attn_wkv': _L0_attn_in['wkv'], 'L0_attn_bkv': _L0_attn_in['bkv'], 'L0_attn_wo': _L0_attn_in['wo'], 'L0_attn_bo': _L0_attn_in['bo'], 'L0_attn_qn_w': _L0_attn_in['qn_w'], 'L0_attn_kn_w': _L0_attn_in['kn_w'], 'L0_ffn_gate_w': _L0_ffn_in['gate_w'], 'L0_ffn_rms_w': _L0_ffn_in['rms_w'], 'L0_ffn_W1': _L0_ffn_in['W1'], 'L0_ffn_W2': _L0_ffn_in['W2'], 'L0_ffn_W3': _L0_ffn_in['W3']}

def reference(x, ctx_1024, L0_attn_wq, L0_attn_bq, L0_attn_wkv, L0_attn_bkv, L0_attn_wo, L0_attn_bo, L0_attn_qn_w, L0_attn_kn_w, L0_ffn_gate_w, L0_ffn_rms_w, L0_ffn_W1, L0_ffn_W2, L0_ffn_W3):
    import jax
    import jax.numpy as jnp

    def _L0_xattn_ref(x, w1, w2):
        import jax, jax.numpy as jnp
        import numpy as np
        E, T, H, F = (8, 256, 128, 512)
        h = jnp.einsum('eth,efh->etf', x, w1)
        a = jax.nn.gelu(h, approximate=True)
        return jnp.einsum('etf,efh->eth', a, w2)

    def _L0_attn_ref(x, wq, bq, wkv, bkv, wo, bo, qn_w, kn_w):
        import jax, jax.numpy as jnp
        import numpy as np
        import math
        D = 128
        H = 16
        HD = D // H
        NKV = H // 4
        SPARSE_K = 64
        TEMP = 1.0
        EPS = 1e-08

        def rmsnorm(x, w):
            return x * jax.lax.rsqrt(jnp.mean(x * x, axis=-1, keepdims=True) + EPS) * w

        def alibi_bias(n_head, T):
            slopes = 2.0 ** (-(jnp.arange(n_head, dtype=jnp.float32) / (n_head - 1) * 8.0))
            pos = jnp.arange(T)
            dist = jnp.abs(pos[:, None] - pos[None, :]).astype(jnp.float32)
            return -slopes[:, None, None] * dist[None, :, :]
        B, T, C = x.shape
        scale = 1.0 / math.sqrt(HD)
        q = (x @ wq + bq).reshape(B, T, H, HD).transpose(0, 2, 1, 3)
        kv = (x @ wkv + bkv).reshape(B, T, 2, NKV, HD)
        k = kv[:, :, 0].transpose(0, 2, 1, 3)
        v = kv[:, :, 1].transpose(0, 2, 1, 3)
        q = rmsnorm(q, qn_w)
        k = rmsnorm(k, kn_w)
        rep = H // NKV
        k = jnp.repeat(k, rep, axis=1)
        v = jnp.repeat(v, rep, axis=1)
        bias = alibi_bias(H, T)
        causal = jnp.triu(jnp.ones((T, T), dtype=bool), 1)
        pre = jnp.einsum('bhqd,bhkd->bhqk', q, k) * scale + bias[None]
        pre = jnp.where(causal, -jnp.inf, pre)
        kk = min(SPARSE_K, T)
        _, topk_idx = jax.lax.top_k(pre, kk)
        bi = jnp.arange(B)[:, None, None, None]
        hi = jnp.arange(H)[None, :, None, None]
        ti = jnp.arange(T)[None, None, :, None]
        sparse_mask = jnp.zeros((B, H, T, T), dtype=bool).at[bi, hi, ti, topk_idx].set(True)
        att = jnp.einsum('bhqd,bhkd->bhqk', q, k) * scale + bias[None]
        att = jnp.where(causal[None, None] | ~sparse_mask, -jnp.inf, att)
        att = jax.nn.softmax(att, axis=-1)
        y = jnp.einsum('bhqk,bhkd->bhqd', att, v)
        y = y.transpose(0, 2, 1, 3).reshape(B, T, C)
        return y @ wo + bo

    def _L0_ffn_ref(x, gate_w, rms_w, W1, W2, W3):
        import jax, jax.numpy as jnp
        import numpy as np
        E, K = (8, 2)
        DM, DE = (128, 352)
        B, S = (1, 256)
        EPS = 1e-06

        def _rmsnorm(x, w):
            var = jnp.mean(jnp.square(x), axis=-1, keepdims=True)
            return x * jax.lax.rsqrt(var + EPS) * w
        y = _rmsnorm(x, rms_w)
        logits = jnp.einsum('bsd,ed->bse', y, gate_w)
        vals, idx = jax.lax.top_k(logits, K)
        w = jax.nn.softmax(vals, axis=-1)
        w_full = jnp.einsum('bsk,bske->bse', w, jax.nn.one_hot(idx, E, dtype=x.dtype))
        up = jnp.einsum('bsd,end->bsen', y, W1)
        gate = jnp.einsum('bsd,end->bsen', y, W2)
        h = jax.nn.silu(up) * gate
        out = jnp.einsum('bsen,emn->bsem', h, W3)
        comb = jnp.einsum('bsem,bse->bsm', out, w_full)
        return x + comb
    x = x + _L0_xattn_ref(_layernorm(x, axis=-1), ctx_1024, ctx_1024)
    x = x + _L0_attn_ref(_layernorm(x, axis=-1), L0_attn_wq, L0_attn_bq, L0_attn_wkv, L0_attn_bkv, L0_attn_wo, L0_attn_bo, L0_attn_qn_w, L0_attn_kn_w)
    x = x + _L0_ffn_ref(_layernorm(x, axis=-1), L0_ffn_gate_w, L0_ffn_rms_w, L0_ffn_W1, L0_ffn_W2, L0_ffn_W3)
    return x

_drawn_inputs = setup_inputs


def setup_inputs(seed=0):
    import zlib

    import numpy as np

    out = dict(_drawn_inputs(seed))
    spreads = {'L0_attn_bq': (0.0, 2.0),
     'L0_attn_bkv': (0.0, 0.407),
     'L0_attn_bo': (0.0, 0.1),
     'L0_attn_qn_w': (1.0, 0.6),
     'L0_attn_kn_w': (1.0, 0.6),
     'L0_ffn_rms_w': (1.0, 0.6)}
    factors = {'L0_attn_wq': 40.051,
     'L0_ffn_gate_w': 42.173,
     'L0_ffn_W1': 39.613,
     'L0_ffn_W2': 39.323,
     'L0_ffn_W3': 39.203,
     'L0_attn_wkv': 2.77}
    for name, (base, spread) in spreads.items():
        noise = np.random.default_rng([zlib.crc32(name.encode()), seed]).standard_normal(out[name].shape)
        drawn = base * np.exp(spread * noise) if base else spread * noise
        out[name] = jnp.asarray(drawn.astype(out[name].dtype))
    for name, factor in factors.items():
        out[name] = (out[name] * factor).astype(out[name].dtype)
    return out
```

```python
from contextlib import ExitStack

import concourse.bass as bass
from concourse import mybir

F32 = mybir.dt.float32
F32R = mybir.dt.float32r
U32 = mybir.dt.uint32
ALU = mybir.AluOpType
ACT = mybir.ActivationFunctionType
AX_X = mybir.AxisListType.X

P = 128
LN_EPS, QK_EPS, RMS_EPS = 1e-5, 1e-8, 1e-6
GELU_CUBIC = 0.044715
GELU_SCALE = 0.7978845608028654

STAGE_SLOT = {
    "norm_x": 0, "latents_t": 1, "cross_scores": 2, "gelu_t": 3, "cross_out": 4,
    "norm_1": 5, "qkv": 6, "head_norm": 8, "scores": 8, "probs": 9, "values": 10, "project": 11,
    "norm_2": 12, "tokens_t": 13, "route": 14, "weights_t": 15,
}
SLOT_STRIDE = 4
FFN_START = 20
FFN_PER_SLOT = 3
SPLIT_START = 16
SPLITS_PER_SLOT = 3
RING = 4
SPLIT = 2


def bass_perceiver_block(nc, x, ctx_rows, ctx_cols, wqkv, bqkv, head_w, wo, bo, gate_w, rms_w, w12_d, w3,
                         ident, score_bias, batch_head_mask, value_mask, expert_ids, out):
    N, D = x.shape
    NB, S = ctx_cols.shape[1], ctx_cols.shape[2]
    T = N // NB
    BT = P // T
    NT = N // P
    SC = S // P
    NKV = value_mask.shape[1]
    KV = wqkv.shape[1] - D >> 1
    HD = KV // NKV
    QK = D + KV
    E = gate_w.shape[1]
    CHUNKS = w12_d.shape[2] // P
    DE = w12_d.shape[2] // E
    HALF = 2 * P
    TPH = HALF // P
    HALVES = N // HALF
    YW = KV + NKV

    plan = [(STAGE_SLOT[s] + SLOT_STRIDE * q, q, n, s) for q in range(NT) for n, s in enumerate(STAGE_SLOT)]
    for i in range(HALVES * CHUNKS):
        first = FFN_START + i // FFN_PER_SLOT
        plan.append((max(first, STAGE_SLOT["weights_t"] + 1 + SLOT_STRIDE * (TPH * (i // CHUNKS + 1) - 1)), NT, i, "expert"))
    for i in range(CHUNKS // SPLIT):
        plan.append((SPLIT_START + i // SPLITS_PER_SLOT, NT + 1, i, "split"))
    plan = [(s, n if s in ("expert", "split") else q) for _, q, n, s in sorted(plan)]

    BANKS = [
        {"cross_scores": "act_done", "scores": "pre_done"},
        {"gelu_t": "actT_done", "probs": "probsT_done", "weights_t": "w_bcast_done"},
        {"latents_t": "xnT0_done", "norm_1": "xn1T_rep_done", "tokens_t": "yT_hi_done"},
        {"cross_out": "x1_done", "qkv": "v_biased", "values": "y_heads_done", "project": "x2_done",
         "route": "logits_copied"},
    ]
    FREED_BY = {}
    for bank in BANKS:
        users = [(stage, q) for stage, q in plan if stage in bank]
        for (before, q0), user in zip(users, users[1:]):
            FREED_BY[user] = bank[before], (2 if before == "weights_t" else 1) * (q0 + 1)

    with ExitStack() as stack:
        def sb(name, shape, dt=F32):
            return stack.enter_context(nc.sbuf_tensor(name, shape, dt))

        def pb(name):
            return stack.enter_context(nc.psum_tensor(name, [P, 512], F32))

        def sem(name):
            return stack.enter_context(nc.semaphore(name))

        x_sb = sb("x_sb", [P, NT, D])
        ctx_r = sb("ctx_r", [P, NB, SC, D])
        ctx_c = sb("ctx_c", [P, NB, S])
        wqkv_sb = sb("wqkv_sb", [P, QK + KV])
        bqkv_sb = sb("bqkv_sb", [P, QK + KV])
        head_sb = sb("head_sb", [P, QK])
        wo_sb = sb("wo_sb", [P, D])
        bo_sb = sb("bo_sb", [P, D])
        gate_sb = sb("gate_sb", [P, E])
        rms_sb = sb("rms_sb", [P, D])
        w12 = sb("w12", [P, RING, 2, SPLIT * P])
        w_bcast = ctx_c[:, 0:E, :]
        w3_sb = ctx_r[:, 0:2 * BT, :, :].rearrange("p b c d -> p (b c) d")[:, 0:CHUNKS, :]
        ident_sb = sb("ident_sb", [P, P])
        bias_sb = sb("bias_sb", [P, NKV, T])
        bh_mask = sb("bh_mask", [P, BT * NKV])
        v_mask = sb("v_mask", [P, NKV])
        ids_sb = sb("ids_sb", [P, E])
        w12_hi = sb("w12_hi", [P, 2, CHUNKS * P], F32R)
        w12_lo = sb("w12_lo", [P, 2, CHUNKS * P], F32R)

        stats = sb("stats", [P, 3, NT, 6])
        mean_var = sb("mean_var", [P, 3, NT, 2])
        var_eps = sb("var_eps", [P, 3, NT])
        rstd = sb("rstd", [P, 3, NT])
        minus_half = sb("minus_half", [P, D // HD + NKV])
        xn = sb("xn", [P, 3, NT, D])
        xnT = sb("xnT", [P, 3, NT, P])
        xn1T_rep = sb("xn1T_rep", [P, 2, BT, NKV, T])
        gelu_rows = sb("gelu_rows", [P, 2, S])
        actT = sb("actT", [P, 2, SC, P])
        x1 = sb("x1", [P, NT, D])
        qk = sb("qk", [P, NT, QK])
        qk_sq = sb("qk_sq", [P, 2, QK])
        qk_ms = sb("qk_ms", [P, NT, QK // HD])
        qk_rs = sb("qk_rs", [P, NT, QK // HD])
        v_biased = sb("v_biased", [P, 2, BT, KV])
        v_all = sb("v_all", [P, NT, BT, YW])
        qkT = sb("qkT", [P, NT, QK])
        k_blocks = sb("k_blocks", [P, 2, BT * NKV, T])
        pre = sb("pre", [P, 2, BT * NKV, T])
        row_max = sb("row_max", [P, NT, BT * NKV])
        probs = sb("probs", [P, 2, BT * NKV, T])
        probsT = sb("probsT", [P, 2, BT, P])
        inv_sum = sb("inv_sum", [P, NT, BT, NKV])
        y_heads = sb("y_heads", [P, NT, BT, KV])
        yT_heads = sb("yT_heads", [P, NT, P])
        x1b = sb("x1b", [P, NT, D])
        x2 = sb("x2", [P, NT, D])
        rms = sb("rms", [P, NT, 4])
        y_tok = sb("y_tok", [P, NT, D])
        yT = sb("yT", [P, N])
        yT_hi = sb("yT_hi", [P, N], F32R)
        yT_lo = sb("yT_lo", [P, N], F32R)
        resid = sb("resid", [P, NT, D])
        top = sb("top", [P, NT, 8])
        top_id = sb("top_id", [P, NT, 8], U32)
        top_idf = sb("top_idf", [P, NT, 2])
        pick = sb("pick", [P, 5, NT])
        diff, ratio, denom, p_first, p_second = (pick[:, k, :] for k in range(5))
        w_first = sb("w_first", [P, NT, E])
        w_second = sb("w_second", [P, NT, E])
        w_full = sb("w_full", [P, NT, E])
        logit_sb = sb("logit_sb", [P, NT, E])
        ffn_t = sb("ffn_t", [P, 2, HALF])
        ffn_u = sb("ffn_u", [P, 2, HALF])
        ffn_v = sb("ffn_v", [P, 3, HALF])
        ffn_h = sb("ffn_h", [P, 3, HALF])
        combT = sb("combT", [P, HALVES, HALF])

        row_ps = pb("row_ps")
        wide_ps = pb("wide_ps")
        small_ps = pb("small_ps")
        outs_ps = pb("outs_ps")
        expert_ps = [pb(f"expert_ps{i}") for i in range(3)]
        comb_ps = pb("comb_ps")

        names = """x_in consts_in attn_in ffn_small_in w3_in
            minus_half_set
            stats0_done stats1_done stats2_done mean0_done mean1_done mean2_done var0_done var1_done var2_done
            rstd0_done rstd1_done rstd2_done xn0_done xn1_done xn2_done xnT0_ps xnT1_ps xnT0_done xnT1_done xn1T_rep_done
            h_done sq_done cubic_done th_done act_done actT_ps actT_done cross_done x1_done
            x1b_done head_w_done sums_set qkv_done qk_done qk_sq_done qk_sum_done qk_ms_done qk_rs_done
            v_biased v_done qk_scaled qk_ready qkT_done k_blocks_done s_done pre_done max_done centred_done
            probs_done probsT_ps probsT_done y_done inv_done y_heads_done yT_heads_done o_done x2_done
            rms_steps rms_done y_tok_done resid_done yT_ps yT_done yT_hi_done yT_lo_done
            logits_done logits_copied top_done top_id_done top_idf_done diff_done exp_done denom_done
            p1_done p2_done w_first_done w_second_done w_full_done w_ps w_bcast_done
            w_hi_done w_lo_done gates_ps tanh_done u_done expert_read h_piece_done down_done
            combT_done out_ps out_ready stored""".split()
        s = {n: sem(n) for n in names}
        w12_in = [sem(f"w12_in{n}") for n in range(RING)]
        ctx_in = [sem(f"ctx_in{q}") for q in range(NT)]
        block = stack.enter_context(nc.Block())

        def batches(q):
            return slice(BT * q, BT * q + BT)

        def tile(q):
            return slice(P * q, P * q + P)

        def half(h):
            return slice(HALF * h, HALF * h + HALF)

        def experts_of(c):
            at, found = 0, []
            while at < P:
                e = (c * P + at) // DE
                n = min((e + 1) * DE - c * P, P) - at
                n = min(n, {0: P, 64: 64}.get(at, 32))
                found.append((e, at, n))
                at += n
            return found

        PIECES = []
        for i in range(HALVES * CHUNKS):
            PIECES.append((PIECES[-1] if PIECES else 0) + len(experts_of(i % CHUNKS)))

        @block.sync
        def _(sp):
            sp.dma_start(x_sb[:], x.rearrange("(q p) d -> p q d", p=P)).then_inc(s["x_in"], 16)
            sp.dma_start(ident_sb[:], ident).then_inc(s["consts_in"], 16)
            for q in range(NT):
                sp.dma_start(ctx_c[:, batches(q), :], ctx_cols[:, batches(q), :]).then_inc(ctx_in[q], 16)
                sp.dma_start(ctx_r[:, batches(q), :, :], ctx_rows[:, batches(q), :, :]).then_inc(ctx_in[q], 16)
                if q == 0:
                    sp.dma_start(wqkv_sb[:], wqkv).then_inc(s["attn_in"], 16)
                    sp.dma_start(bqkv_sb[:], bqkv.partition_broadcast(P)).then_inc(s["attn_in"], 16)
                    sp.dma_start(head_sb[:], head_w.partition_broadcast(P)).then_inc(s["attn_in"], 16)
                    sp.dma_start(wo_sb[:], wo).then_inc(s["attn_in"], 16)
                    sp.dma_start(bo_sb[:], bo.partition_broadcast(P)).then_inc(s["attn_in"], 16)
                    sp.dma_start(bias_sb[:], score_bias).then_inc(s["attn_in"], 16)
                    sp.dma_start(bh_mask[:], batch_head_mask).then_inc(s["attn_in"], 16)
                    sp.dma_start(v_mask[:], value_mask).then_inc(s["attn_in"], 16)
                    sp.dma_start(gate_sb[:], gate_w).then_inc(s["ffn_small_in"], 16)
                    sp.dma_start(rms_sb[:], rms_w.partition_broadcast(P)).then_inc(s["ffn_small_in"], 16)
                    sp.dma_start(ids_sb[:], expert_ids.partition_broadcast(P)).then_inc(s["ffn_small_in"], 16)
            for n in range(CHUNKS // SPLIT):
                if n >= RING:
                    sp.wait_ge(s["w_lo_done"], n - RING + 1)
                sp.dma_start(w12[:, n % RING, :, :], w12_d[:, :, n * SPLIT * P:(n + 1) * SPLIT * P]).then_inc(w12_in[n % RING], 16)
                if n == RING - 1:
                    sp.wait_ge(s["cross_done"], 2)
                    sp.dma_start(w3_sb, w3).then_inc(s["w3_in"], 16)
            out_v = out.rearrange("(q p) d -> q p d", p=P)
            for q in range(NT):
                sp.wait_ge(s["out_ready"], q + 1)
                sp.dma_start(out_v[q], resid[:, q, :]).then_inc(s["stored"], 16)
            sp.wait_ge(s["stored"], 16 * NT)

        ATTN_IN, FFN_SMALL_IN = 16 * 8, 16 * 3

        @block.tensor
        def _(pe):
            pe.wait_ge(s["consts_in"], 16)

            def bank_free(stage, q):
                if (stage, q) in FREED_BY:
                    signal, count = FREED_BY[stage, q]
                    pe.wait_ge(s[signal], count)

            def transpose_rows(q, src, src_ready, done, stage):
                pe.wait_ge(src_ready, q + 1)
                bank_free(stage, q)
                pe.transpose(small_ps[:, 0:P], src, ident_sb[:]).then_inc(done, 1)

            def down(i):
                h, c = divmod(i, CHUNKS)
                pe.wait_ge(s["h_piece_done"], PIECES[i])
                if i == 0:
                    pe.wait_ge(s["w3_in"], 16)
                if c == 0 and h:
                    pe.wait_ge(s["combT_done"], h)
                pe.matmul(comb_ps[:, 0:HALF], w3_sb[:, c, :], ffn_h[:, i % 3, :],
                          start=(c == 0), stop=(c == CHUNKS - 1)).then_inc(s["down_done"], 1)

            for stage, q in plan:
                if stage == "latents_t":
                    transpose_rows(q, xn[:, 0, q, :], s["xn0_done"], s["xnT0_ps"], stage)
                elif stage == "cross_scores":
                    pe.wait_ge(s["xnT0_done"], q + 1)
                    pe.wait_ge(ctx_in[q], 32)
                    bank_free(stage, q)
                    for j in range(BT):
                        mm = pe.matmul(row_ps[T * j:T * j + T, 0:S], xnT[:, 0, q, T * j:T * j + T],
                                       ctx_c[:, BT * q + j, :], start=True, stop=True)
                    mm.then_inc(s["h_done"], 1)
                elif stage == "gelu_t":
                    pe.wait_ge(s["act_done"], q + 1)
                    bank_free(stage, q)
                    for c in range(SC):
                        mm = pe.transpose(wide_ps[:, c * P:c * P + P], gelu_rows[:, q % 2, c * P:c * P + P], ident_sb[:])
                    mm.then_inc(s["actT_ps"], 1)
                elif stage == "cross_out":
                    pe.wait_ge(s["actT_done"], q + 1)
                    bank_free(stage, q)
                    for c in range(SC):
                        for j in range(BT):
                            mm = pe.matmul(outs_ps[T * j:T * j + T, 0:D], actT[:, q % 2, c, T * j:T * j + T],
                                           ctx_r[:, BT * q + j, c, :], start=(c == 0), stop=(c == SC - 1),
                                           skip_group_check=True)
                    mm.then_inc(s["cross_done"], 1)
                elif stage == "norm_1":
                    transpose_rows(q, xn[:, 1, q, :], s["xn1_done"], s["xnT1_ps"], stage)
                elif stage == "qkv":
                    pe.wait_ge(s["xnT1_done"], q + 1)
                    pe.wait_ge(s["attn_in"], ATTN_IN)
                    bank_free(stage, q)
                    pe.matmul(outs_ps[:, 0:QK], xnT[:, 1, q, :], wqkv_sb[:, 0:QK], start=True, stop=True)
                    pe.wait_ge(s["xn1T_rep_done"], q + 1)
                    for j in range(BT):
                        rows = xn1T_rep[:, q % 2, j, :, :].rearrange("p g t -> p (g t)")
                        mm = pe.matmul(outs_ps[:, QK + KV * j:QK + KV * j + KV], rows, wqkv_sb[:, QK:QK + KV],
                                       start=True, stop=True)
                    mm.then_inc(s["qkv_done"], 1)
                elif stage == "scores":
                    pe.wait_ge(s["k_blocks_done"], q + 1)
                    bank_free(stage, q)
                    pe.matmul(row_ps[:, :], qkT[:, q, 0:D], k_blocks[:, q % 2, :, :].rearrange("p a t -> p (a t)"),
                              start=True, stop=True).then_inc(s["s_done"], 1)
                elif stage == "probs":
                    pe.wait_ge(s["probs_done"], q + 1)
                    bank_free(stage, q)
                    for j in range(BT):
                        rows = probs[:, q % 2, NKV * j:NKV * j + NKV, :].rearrange("p a t -> p (a t)")
                        mm = pe.transpose(wide_ps[:, P * j:P * j + P], rows, ident_sb[:])
                    mm.then_inc(s["probsT_ps"], 1)
                elif stage == "values":
                    pe.wait_ge(s["probsT_done"], q + 1)
                    pe.wait_ge(s["v_done"], q + 1)
                    bank_free(stage, q)
                    for j in range(BT):
                        mm = pe.matmul(outs_ps[:, YW * j:YW * j + YW], probsT[:, q % 2, j, :], v_all[:, q, j, :],
                                       start=True, stop=True)
                    mm.then_inc(s["y_done"], 1)
                elif stage == "project":
                    pe.wait_ge(s["yT_heads_done"], q + 1)
                    bank_free(stage, q)
                    pe.matmul(outs_ps[:, 0:D], yT_heads[:, q, :], wo_sb[:], start=True, stop=True).then_inc(s["o_done"], 1)
                elif stage == "tokens_t":
                    transpose_rows(q, y_tok[:, q, :], s["y_tok_done"], s["yT_ps"], stage)
                elif stage == "route":
                    pe.wait_ge(s["yT_done"], q + 1)
                    pe.wait_ge(s["ffn_small_in"], FFN_SMALL_IN)
                    bank_free(stage, q)
                    pe.matmul(outs_ps[:, 0:E], yT[:, tile(q)], gate_sb[:], start=True, stop=True).then_inc(s["logits_done"], 1)
                elif stage == "weights_t":
                    pe.wait_ge(s["w_full_done"], q + 1)
                    for part in range(2):
                        if part == 0:
                            bank_free(stage, q)
                        else:
                            pe.wait_ge(s["w_bcast_done"], 2 * q + 1)
                        for k in range(E // 2):
                            e = part * (E // 2) + k
                            mm = pe.matmul(wide_ps[:, P * k:P * k + P], w_full[:, q, e:e + 1].broadcast_to([P, P]),
                                           ident_sb[:], start=True, stop=True)
                        mm.then_inc(s["w_ps"], 1)
                elif stage == "expert":
                    i = q
                    h, c = divmod(i, CHUNKS)
                    if c == 0:
                        pe.wait_ge(s["yT_hi_done"], TPH * (h + 1))
                        pe.wait_ge(s["yT_lo_done"], TPH * (h + 1))
                    if h == 0:
                        pe.wait_ge(s["w_lo_done"], c // SPLIT + 1)
                    if i >= 3:
                        pe.wait_ge(s["expert_read"], i - 2)
                    cols = slice(c * P, c * P + P)
                    for k in range(2):
                        o = expert_ps[i % 3][:, HALF * k:HALF * k + HALF]
                        pe.matmul(o, w12_hi[:, k, cols], yT_hi[:, half(h)], start=True, stop=False)
                        pe.matmul(o, w12_hi[:, k, cols], yT_lo[:, half(h)], start=False, stop=False)
                        mm = pe.matmul(o, w12_lo[:, k, cols], yT_hi[:, half(h)], start=False, stop=True)
                    mm.then_inc(s["gates_ps"], 1)
                    if i >= 2:
                        down(i - 2)
            for i in range(HALVES * CHUNKS - 2, HALVES * CHUNKS):
                down(i)
            for q in range(NT):
                pe.wait_ge(s["combT_done"], q // TPH + 1)
                bank = expert_ps[q % 3]
                if q >= 3:
                    pe.wait_ge(s["out_ready"], q - 2)
                else:
                    pe.wait_ge(s["expert_read"], HALVES * CHUNKS)
                pe.transpose(bank[:, 0:P], combT[:, q // TPH, P * (q % TPH):P * (q % TPH) + P],
                             ident_sb[:]).then_inc(s["out_ps"], 1)

        @block.scalar
        def _(act):
            for stage, q in plan:
                if stage == "latents_t":
                    act.wait_ge(s["xnT0_ps"], q + 1)
                    act.activation(xnT[:, 0, q, :], small_ps[:, 0:P], ACT.Copy).then_inc(s["xnT0_done"], 1)
                elif stage == "cross_scores":
                    act.wait_ge(s["h_done"], q + 1)
                    if q >= 2:
                        act.wait_ge(s["actT_ps"], q - 1)
                    act.activation(gelu_rows[:, q % 2, :], row_ps[:, :], ACT.Square).then_inc(s["sq_done"], 1)
                    act.wait_ge(s["cubic_done"], q + 1)
                    act.activation(gelu_rows[:, q % 2, :], gelu_rows[:, q % 2, :], ACT.Tanh,
                                   scale=GELU_SCALE * GELU_CUBIC).then_inc(s["th_done"], 1)
                elif stage == "gelu_t":
                    act.wait_ge(s["actT_ps"], q + 1)
                    if q >= 2:
                        act.wait_ge(s["cross_done"], q - 1)
                    act.activation(actT[:, q % 2, :, :].rearrange("p c t -> p (c t)"), wide_ps[:, :],
                                   ACT.Copy).then_inc(s["actT_done"], 1)
                elif stage == "norm_1":
                    act.wait_ge(s["xnT1_ps"], q + 1)
                    act.activation(xnT[:, 1, q, :], small_ps[:, 0:P], ACT.Copy).then_inc(s["xnT1_done"], 1)
                    if q >= 2:
                        act.wait_ge(s["qkv_done"], q - 1)
                    act.activation(xn1T_rep[:, q % 2, :, :, :],
                                   small_ps[:, 0:P].rearrange("p (b t) -> p b t", t=T).unsqueeze(2).broadcast_to([P, BT, NKV, T]),
                                   ACT.Copy).then_inc(s["xn1T_rep_done"], 1)
                elif stage == "scores":
                    act.wait_ge(s["centred_done"], q + 1)
                    if q >= 2:
                        act.wait_ge(s["probsT_ps"], q - 1)
                    act.activation(probs[:, q % 2, :, :], pre[:, q % 2, :, :], ACT.Exp).then_inc(s["probs_done"], 1)
                elif stage == "probs":
                    act.wait_ge(s["probsT_ps"], q + 1)
                    if q >= 2:
                        act.wait_ge(s["y_done"], q - 1)
                    act.activation(probsT[:, q % 2, :, :].rearrange("p c t -> p (c t)"), wide_ps[:, :],
                                   ACT.Copy).then_inc(s["probsT_done"], 1)
                elif stage == "tokens_t":
                    act.wait_ge(s["yT_ps"], q + 1)
                    act.activation(yT[:, tile(q)], small_ps[:, 0:P], ACT.Copy).then_inc(s["yT_done"], 1)
                    act.activation(yT_hi[:, tile(q)], small_ps[:, 0:P], ACT.Copy).then_inc(s["yT_hi_done"], 1)
                elif stage == "route":
                    act.wait_ge(s["diff_done"], q + 1)
                    act.activation(ratio[:, q:q + 1], diff[:, q:q + 1], ACT.Exp).then_inc(s["exp_done"], 1)
                elif stage == "weights_t":
                    for part in range(2):
                        e = part * (E // 2)
                        act.wait_ge(s["w_ps"], 2 * q + part + 1)
                        act.wait_ge(s["h_done"], 2)
                        act.activation(w_bcast[:, e:e + E // 2, tile(q)],
                                       wide_ps[:, :].rearrange("p (e t) -> p e t", t=P), ACT.Copy,
                                       scale=0.5).then_inc(s["w_bcast_done"], 1)
                elif stage == "split":
                    cols = slice(q * SPLIT * P, (q + 1) * SPLIT * P)
                    act.wait_ge(w12_in[q % RING], 16 * (q // RING + 1))
                    act.activation(w12_hi[:, :, cols], w12[:, q % RING, :, :], ACT.Copy).then_inc(s["w_hi_done"], 1)
                elif stage == "expert":
                    i = q
                    act.wait_ge(s["gates_ps"], i + 1)
                    if i >= 2:
                        act.wait_ge(s["u_done"], i - 1)
                    act.activation(ffn_t[:, i % 2, :], expert_ps[i % 3][:, 0:HALF], ACT.Tanh,
                                   scale=0.5).then_inc(s["tanh_done"], 1)
                    h, c = divmod(i, CHUNKS)
                    if h and c == 1:
                        act.wait_ge(s["down_done"], CHUNKS * h)
                        act.activation(combT[:, h - 1, :], comb_ps[:, 0:HALF], ACT.Copy).then_inc(s["combT_done"], 1)
            act.wait_ge(s["down_done"], CHUNKS * HALVES)
            act.activation(combT[:, HALVES - 1, :], comb_ps[:, 0:HALF], ACT.Copy).then_inc(s["combT_done"], 1)

        @block.gpsimd
        def _(pool):
            pieces = 0
            pool.memset(minus_half[:], -0.5).then_inc(s["minus_half_set"], 1)
            pool.wait_ge(s["minus_half_set"], 1)

            def rsqrt_var(k, q):
                pool.wait_ge(s[f"var{k}_done"], q + 1)
                pool.tensor_tensor(rstd[:, k, q:q + 1], var_eps[:, k, q:q + 1], minus_half[:, 0:1],
                                   ALU.pow).then_inc(s[f"rstd{k}_done"], 1)

            for stage, q in plan:
                if stage == "norm_x":
                    rsqrt_var(0, q)
                elif stage == "cross_out":
                    rsqrt_var(1, q)
                    pool.wait_ge(s["x1_done"], q + 1)
                    pool.wait_ge(s["attn_in"], ATTN_IN)
                    pool.tensor_tensor(x1b[:, q, :], x1[:, q, :], bo_sb[:], ALU.add).then_inc(s["x1b_done"], 1)
                elif stage == "qkv":
                    pool.wait_ge(s["qk_ms_done"], q + 1)
                    pool.tensor_tensor(qk_rs[:, q, :], qk_ms[:, q, :], minus_half[:, 0:QK // HD],
                                       ALU.pow).then_inc(s["qk_rs_done"], 1)
                elif stage == "project":
                    rsqrt_var(2, q)
                    r, v, m = rstd[:, 2, q:q + 1], mean_var[:, 2, q, 1:2], [rms[:, q, k:k + 1] for k in range(4)]
                    pool.wait_ge(s["rstd2_done"], q + 1)
                    pool.tensor_tensor(m[0], r, r, ALU.mult).then_inc(s["rms_steps"], 1)
                    pool.wait_ge(s["rms_steps"], 3 * q + 1)
                    pool.tensor_tensor(m[1], m[0], v, ALU.mult).then_inc(s["rms_steps"], 1)
                    pool.wait_ge(s["rms_steps"], 3 * q + 2)
                    pool.tensor_scalar(m[2], m[1], RMS_EPS, None, ALU.add).then_inc(s["rms_steps"], 1)
                    pool.wait_ge(s["rms_steps"], 3 * q + 3)
                    pool.tensor_tensor(m[3], m[2], minus_half[:, 0:1], ALU.pow).then_inc(s["rms_done"], 1)
                elif stage == "norm_2":
                    pool.wait_ge(s["xn2_done"], q + 1)
                    pool.tensor_tensor(resid[:, q, :], x2[:, q, :], xn[:, 2, q, :], ALU.add).then_inc(s["resid_done"], 1)
                elif stage == "tokens_t":
                    pool.wait_ge(s["yT_hi_done"], q + 1)
                    pool.tensor_tensor(yT_lo[:, tile(q)], yT[:, tile(q)], yT_hi[:, tile(q)].bitcast(F32),
                                       ALU.subtract).then_inc(s["yT_lo_done"], 1)
                elif stage == "split":
                    cols = slice(q * SPLIT * P, (q + 1) * SPLIT * P)
                    pool.wait_ge(s["w_hi_done"], q + 1)
                    pool.tensor_tensor(w12_lo[:, :, cols], w12[:, q % RING, :, :], w12_hi[:, :, cols].bitcast(F32),
                                       ALU.subtract).then_inc(s["w_lo_done"], 1)
                elif stage == "expert":
                    i = q
                    h, c = divmod(i, CHUNKS)
                    pool.wait_ge(s["expert_read"], i + 1)
                    if c == 0:
                        pool.wait_ge(s["w_bcast_done"], 2 * TPH * (h + 1))
                    if i >= 3:
                        pool.wait_ge(s["down_done"], i - 2)
                    for e, at, n in experts_of(c):
                        rows = slice(at, at + n)
                        pool.tensor_tensor(ffn_h[rows, i % 3, :], ffn_v[rows, i % 3, :],
                                           w_bcast[rows, e, half(h)], ALU.mult).then_inc(s["h_piece_done"], 1)
                        pieces += 1
                        if n < P:
                            pool.wait_ge(s["h_piece_done"], pieces)

        @block.vector
        def _(dve):
            def row_stats(k, q, src):
                dve.bn_stats(stats[:, k, q, :], src).then_inc(s[f"stats{k}_done"], 1)
                dve.wait_ge(s[f"stats{k}_done"], q + 1)
                dve.bn_aggr(mean_var[:, k, q, :], stats[:, k, q, :]).then_inc(s[f"mean{k}_done"], 1)
                dve.wait_ge(s[f"mean{k}_done"], q + 1)
                dve.tensor_scalar(var_eps[:, k, q:q + 1], mean_var[:, k, q, 1:2], LN_EPS, None,
                                  ALU.add).then_inc(s[f"var{k}_done"], 1)

            def normalise(k, q, src):
                dve.wait_ge(s[f"rstd{k}_done"], q + 1)
                dve.tensor_scalar(xn[:, k, q, :], src, mean_var[:, k, q, 0:1], rstd[:, k, q:q + 1],
                                  ALU.subtract, ALU.mult).then_inc(s[f"xn{k}_done"], 1)

            dve.wait_ge(s["x_in"], 16)
            for stage, q in plan:
                if stage == "norm_x":
                    row_stats(0, q, x_sb[:, q, :])
                elif stage == "latents_t":
                    normalise(0, q, x_sb[:, q, :])
                elif stage == "cross_scores":
                    dve.wait_ge(s["sq_done"], q + 1)
                    dve.scalar_tensor_tensor(out=gelu_rows[:, q % 2, :], in0=gelu_rows[:, q % 2, :], scalar=1.0 / GELU_CUBIC,
                                             in1=row_ps[:, :], op0=ALU.add, op1=ALU.mult).then_inc(s["cubic_done"], 1)
                elif stage == "gelu_t":
                    dve.wait_ge(s["th_done"], q + 1)
                    dve.scalar_tensor_tensor(out=gelu_rows[:, q % 2, :], in0=gelu_rows[:, q % 2, :], scalar=1.0,
                                             in1=row_ps[:, :], op0=ALU.add,
                                             op1=ALU.mult).then_inc(s["act_done"], 1)
                elif stage == "cross_out":
                    dve.wait_ge(s["cross_done"], q + 1)
                    dve.scalar_tensor_tensor(out=x1[:, q, :], in0=outs_ps[:, 0:D], scalar=0.5, in1=x_sb[:, q, :],
                                             op0=ALU.mult, op1=ALU.add).then_inc(s["x1_done"], 1)
                    dve.wait_ge(s["x1_done"], q + 1)
                    row_stats(1, q, x1[:, q, :])
                elif stage == "norm_1":
                    normalise(1, q, x1[:, q, :])
                elif stage == "qkv":
                    if q == 0:
                        dve.wait_ge(s["attn_in"], ATTN_IN)
                        dve.tensor_scalar(head_sb[:, 0:D], head_sb[:, 0:D], float(HD) ** -0.5, None,
                                          ALU.mult).then_inc(s["head_w_done"], 1)
                        dve.tensor_copy(v_all[:, :, :, KV:YW].rearrange("p q b g -> p (q b) g"),
                                        v_mask[:].unsqueeze(1).broadcast_to([P, NT * BT, NKV])).then_inc(s["sums_set"], 1)
                    dve.wait_ge(s["qkv_done"], q + 1)
                    dve.tensor_tensor(qk[:, q, :], outs_ps[:, 0:QK], bqkv_sb[:, 0:QK], ALU.add).then_inc(s["qk_done"], 1)
                    if q >= 2:
                        dve.wait_ge(s["v_done"], q - 1)
                    dve.tensor_tensor(v_biased[:, q % 2, :, :],
                                      outs_ps[:, QK:QK + BT * KV].rearrange("p (b v) -> p b v", v=KV),
                                      bqkv_sb[:, QK:QK + KV].unsqueeze(1).broadcast_to([P, BT, KV]),
                                      ALU.add).then_inc(s["v_biased"], 1)
                    dve.wait_ge(s["qk_done"], q + 1)
                    dve.tensor_tensor(qk_sq[:, q % 2, :], qk[:, q, :], qk[:, q, :], ALU.mult).then_inc(s["qk_sq_done"], 1)
                    dve.wait_ge(s["qk_sq_done"], q + 1)
                    dve.tensor_reduce(qk_ms[:, q, :], qk_sq[:, q % 2, :].rearrange("p (h d) -> p h d", d=HD),
                                      AX_X, ALU.add).then_inc(s["qk_sum_done"], 1)
                    dve.wait_ge(s["qk_sum_done"], q + 1)
                    dve.tensor_scalar(qk_ms[:, q, :], qk_ms[:, q, :], 1.0 / HD, QK_EPS, ALU.mult,
                                      ALU.add).then_inc(s["qk_ms_done"], 1)
                    dve.wait_ge(s["v_biased"], q + 1)
                    dve.wait_ge(s["sums_set"], 1)
                    dve.tensor_tensor(v_all[:, q, :, 0:KV].rearrange("p b (g d) -> p b g d", g=NKV),
                                      v_biased[:, q % 2, :, :].rearrange("p b (g d) -> p b g d", g=NKV),
                                      v_mask[:].unsqueeze(1).unsqueeze(3).broadcast_to([P, BT, NKV, HD]),
                                      ALU.mult).then_inc(s["v_done"], 1)
                elif stage == "head_norm":
                    dve.wait_ge(s["qk_rs_done"], q + 1)
                    dve.wait_ge(s["head_w_done"], 1)
                    heads = qk[:, q, :].rearrange("p (h d) -> p h d", d=HD)
                    dve.tensor_tensor(heads, heads, qk_rs[:, q, :].unsqueeze(2).broadcast_to([P, QK // HD, HD]),
                                      ALU.mult).then_inc(s["qk_scaled"], 1)
                    dve.wait_ge(s["qk_scaled"], q + 1)
                    dve.tensor_tensor(qk[:, q, :], qk[:, q, :], head_sb[:], ALU.mult).then_inc(s["qk_ready"], 1)
                    dve.wait_ge(s["qk_ready"], q + 1)
                    dve.transpose(qkT[:, q, :], qk[:, q, :]).then_inc(s["qkT_done"], 1)
                    dve.wait_ge(s["qkT_done"], q + 1)
                    if q >= 2:
                        dve.wait_ge(s["s_done"], q - 1)
                    dve.tensor_tensor(k_blocks[:, q % 2, :, :],
                                      qkT[:, q, D:QK].unsqueeze(1).broadcast_to([P, BT * NKV, T]),
                                      bh_mask[:].unsqueeze(2).broadcast_to([P, BT * NKV, T]),
                                      ALU.mult).then_inc(s["k_blocks_done"], 1)
                elif stage == "scores":
                    dve.wait_ge(s["s_done"], q + 1)
                    if q >= 2:
                        dve.wait_ge(s["probs_done"], q - 1)
                    flat = pre[:, q % 2, :, :].rearrange("p (b g) t -> p b (g t)", g=NKV)
                    dve.tensor_tensor(flat, row_ps[:, :].rearrange("p (b n) -> p b n", b=BT),
                                      bias_sb[:].rearrange("p g t -> p (g t)").unsqueeze(1).broadcast_to([P, BT, NKV * T]),
                                      ALU.add).then_inc(s["pre_done"], 1)
                    dve.wait_ge(s["pre_done"], q + 1)
                    dve.tensor_reduce(row_max[:, q, :], pre[:, q % 2, :, :], AX_X, ALU.max).then_inc(s["max_done"], 1)
                    dve.wait_ge(s["max_done"], q + 1)
                    dve.tensor_tensor(pre[:, q % 2, :, :], pre[:, q % 2, :, :],
                                      row_max[:, q, :].unsqueeze(2).broadcast_to([P, BT * NKV, T]),
                                      ALU.subtract).then_inc(s["centred_done"], 1)
                elif stage == "values":
                    y = outs_ps[:, 0:BT * YW].rearrange("p (b n) -> p b n", n=YW)
                    dve.wait_ge(s["y_done"], q + 1)
                    dve.reciprocal(inv_sum[:, q, :, :], y[:, :, KV:YW]).then_inc(s["inv_done"], 1)
                    dve.wait_ge(s["inv_done"], q + 1)
                    dve.tensor_tensor(y_heads[:, q, :, :].rearrange("p b (g d) -> p b g d", g=NKV),
                                      y[:, :, 0:KV].rearrange("p b (g d) -> p b g d", g=NKV),
                                      inv_sum[:, q, :, :].unsqueeze(3).broadcast_to([P, BT, NKV, HD]),
                                      ALU.mult).then_inc(s["y_heads_done"], 1)
                    dve.wait_ge(s["y_heads_done"], q + 1)
                    dve.transpose(yT_heads[:, q, :], y_heads[:, q, :, :].rearrange("p b v -> p (b v)")).then_inc(s["yT_heads_done"], 1)
                elif stage == "project":
                    dve.wait_ge(s["o_done"], q + 1)
                    dve.wait_ge(s["x1b_done"], q + 1)
                    dve.tensor_tensor(x2[:, q, :], outs_ps[:, 0:D], x1b[:, q, :], ALU.add).then_inc(s["x2_done"], 1)
                    dve.wait_ge(s["x2_done"], q + 1)
                    row_stats(2, q, x2[:, q, :])
                elif stage == "norm_2":
                    normalise(2, q, x2[:, q, :])
                    dve.wait_ge(s["xn2_done"], q + 1)
                    dve.wait_ge(s["rms_done"], q + 1)
                    dve.wait_ge(s["ffn_small_in"], FFN_SMALL_IN)
                    dve.scalar_tensor_tensor(out=y_tok[:, q, :], in0=xn[:, 2, q, :], scalar=rms[:, q, 3:4],
                                             in1=rms_sb[:], op0=ALU.mult, op1=ALU.mult).then_inc(s["y_tok_done"], 1)
                elif stage == "route":
                    one = slice(q, q + 1)
                    dve.wait_ge(s["logits_done"], q + 1)
                    dve.tensor_copy(logit_sb[:, q, :], outs_ps[:, 0:E]).then_inc(s["logits_copied"], 1)
                    dve.wait_ge(s["logits_copied"], q + 1)
                    dve.max(top[:, q, :], logit_sb[:, q, :]).then_inc(s["top_done"], 1)
                    dve.wait_ge(s["top_done"], q + 1)
                    dve.tensor_tensor(diff[:, one], top[:, q, 1:2], top[:, q, 0:1], ALU.subtract).then_inc(s["diff_done"], 1)
                    dve.max_index(top_id[:, q, :], top[:, q, :], logit_sb[:, q, :]).then_inc(s["top_id_done"], 1)
                    dve.wait_ge(s["top_id_done"], q + 1)
                    dve.tensor_copy(top_idf[:, q, :], top_id[:, q, 0:2]).then_inc(s["top_idf_done"], 1)
                    dve.wait_ge(s["exp_done"], q + 1)
                    dve.tensor_scalar(denom[:, one], ratio[:, one], 1.0, None, ALU.add).then_inc(s["denom_done"], 1)
                    dve.wait_ge(s["denom_done"], q + 1)
                    dve.reciprocal(p_first[:, one], denom[:, one]).then_inc(s["p1_done"], 1)
                    dve.wait_ge(s["p1_done"], q + 1)
                    dve.tensor_tensor(p_second[:, one], ratio[:, one], p_first[:, one], ALU.mult).then_inc(s["p2_done"], 1)
                    dve.wait_ge(s["top_idf_done"], q + 1)
                    dve.tensor_scalar(w_first[:, q, :], ids_sb[:], top_idf[:, q, 0:1], p_first[:, one],
                                      ALU.is_equal, ALU.mult).then_inc(s["w_first_done"], 1)
                    dve.wait_ge(s["p2_done"], q + 1)
                    dve.tensor_scalar(w_second[:, q, :], ids_sb[:], top_idf[:, q, 1:2], p_second[:, one],
                                      ALU.is_equal, ALU.mult).then_inc(s["w_second_done"], 1)
                    dve.wait_ge(s["w_first_done"], q + 1)
                    dve.wait_ge(s["w_second_done"], q + 1)
                    dve.tensor_tensor(w_full[:, q, :], w_first[:, q, :], w_second[:, q, :], ALU.add).then_inc(s["w_full_done"], 1)
                elif stage == "expert":
                    i = q
                    up, gate = expert_ps[i % 3][:, 0:HALF], expert_ps[i % 3][:, HALF:2 * HALF]
                    dve.wait_ge(s["tanh_done"], i + 1)
                    dve.scalar_tensor_tensor(out=ffn_u[:, i % 2, :], in0=ffn_t[:, i % 2, :], scalar=1.0, in1=up,
                                             op0=ALU.add, op1=ALU.mult).then_inc(s["u_done"], 1)
                    dve.wait_ge(s["u_done"], i + 1)
                    if i >= 3:
                        dve.wait_ge(s["h_piece_done"], PIECES[i - 3])
                    dve.tensor_tensor(ffn_v[:, i % 3, :], ffn_u[:, i % 2, :], gate, ALU.mult).then_inc(s["expert_read"], 1)
            for q in range(NT):
                dve.wait_ge(s["out_ps"], q + 1)
                dve.wait_ge(s["resid_done"], q + 1)
                dve.tensor_tensor(resid[:, q, :], resid[:, q, :], expert_ps[q % 3][:, 0:P], ALU.add).then_inc(s["out_ready"], 1)


def kernel(x, ctx_1024, L0_attn_wq, L0_attn_bq, L0_attn_wkv, L0_attn_bkv, L0_attn_wo, L0_attn_bo,
           L0_attn_qn_w, L0_attn_kn_w, L0_ffn_gate_w, L0_ffn_rms_w, L0_ffn_W1, L0_ffn_W2, L0_ffn_W3):
    import numpy as np
    import concourse.bacc as bacc
    from concourse.bass_utils import run_bass_kernel_spmd

    x, ctx = np.asarray(x), np.asarray(ctx_1024)
    NB, T, D = x.shape
    S = ctx.shape[1]
    HD = L0_attn_qn_w.shape[0]
    H = D // HD
    KV = L0_attn_wkv.shape[1] // 2
    NKV = KV // HD
    REP = H // NKV
    E, DE = L0_ffn_W1.shape[:2]
    BT = P // T
    f32 = np.float32

    def grouped(a):
        a = np.asarray(a)
        return a.reshape(a.shape[:-1] + (NKV, REP, HD)).swapaxes(-3, -2).reshape(a.shape)

    part = np.arange(P)
    slopes = (2.0 ** (-(np.arange(H, dtype=f32) / f32(H - 1) * f32(8.0)))).astype(f32)
    head = np.arange(NKV)[None, :] * REP + (part // T)[:, None]
    dist = ((part % T)[:, None] - np.arange(T)[None, :])[:, None, :]
    score_bias = np.where(dist < 0, f32(-1e30), -slopes[head][:, :, None] * np.abs(dist).astype(f32)).astype(f32)
    batch_head_mask = ((part // HD)[:, None] == np.arange(BT * NKV)[None, :]).astype(f32)
    value_mask = ((part // T)[:, None] == np.arange(NKV)[None, :]).astype(f32)

    arrays = {
        "x": x.reshape(NB * T, D),
        "ctx_rows": ctx.reshape(NB, S // P, P, D).transpose(2, 0, 1, 3),
        "ctx_cols": ctx.transpose(2, 0, 1),
        "wqkv": np.concatenate([grouped(L0_attn_wq), np.asarray(L0_attn_wkv)], axis=1),
        "bqkv": np.concatenate([grouped(L0_attn_bq), np.asarray(L0_attn_bkv)]),
        "head_w": np.concatenate([np.tile(np.asarray(L0_attn_qn_w), H), np.tile(np.asarray(L0_attn_kn_w), NKV)]),
        "wo": np.ascontiguousarray(grouped(np.asarray(L0_attn_wo).T).T),
        "bo": np.asarray(L0_attn_bo),
        "gate_w": np.asarray(L0_ffn_gate_w).T,
        "rms_w": np.asarray(L0_ffn_rms_w),
        "w12": np.stack([np.asarray(w).reshape(E * DE, D).T for w in (L0_ffn_W1, L0_ffn_W2)], axis=1),
        "w3": np.asarray(L0_ffn_W3).transpose(0, 2, 1).reshape(E * DE // P, P, D).transpose(1, 0, 2),
        "ident": np.eye(P, dtype=f32),
        "score_bias": score_bias,
        "batch_head_mask": batch_head_mask,
        "value_mask": value_mask,
        "expert_ids": np.arange(E, dtype=f32),
    }
    arrays = {f"in_{n}": np.ascontiguousarray(a) for n, a in arrays.items()}
    nc = bacc.Bacc("TRN2", target_bir_lowering=False, num_devices=1)
    args = [nc.dram_tensor(n, a.shape, F32, kind="ExternalInput").ap() for n, a in arrays.items()]
    args.append(nc.dram_tensor("out_0", (NB * T, D), F32, kind="ExternalOutput").ap())
    bass_perceiver_block(nc, *args)
    r = run_bass_kernel_spmd(nc, [arrays], core_ids=[0])
    return r.results[0]["out_0"].reshape(NB, T, D)
```

```python
from contextlib import ExitStack

import concourse.bass as bass
from concourse import mybir

F32 = mybir.dt.float32
F32R = mybir.dt.float32r
U32 = mybir.dt.uint32
ALU = mybir.AluOpType
ACT = mybir.ActivationFunctionType
AX_X = mybir.AxisListType.X

P = 128
LN_EPS, QK_EPS, RMS_EPS = 1e-5, 1e-8, 1e-6
GELU_CUBIC = 0.044715
GELU_SCALE = 0.7978845608028654

STAGE_SLOT = {
    "tensor": {"latents_t": 1, "cross_scores": 2, "gelu_t": 3, "cross_out": 4, "norm_1": 5, "qkv": 5.79,
        "scores": 8, "probs": 9.01, "values": 10, "project": 11, "tokens_t": 13, "route": 14, "weights_t": 15},
    "vector": {"norm_x": 0, "latents_t": 0.67, "cross_scores": 2.25, "gelu_t": 3, "cross_out": 4, "norm_1": 5,
        "qkv": 5.79, "head_norm": 7.51, "scores": 8, "value_rows": 8.85, "values": 10, "project": 11,
        "norm_2": 12, "route": 14, "route_weights": 14.23, "weights_t": 15},
    "scalar": {"latents_t": 1, "cross_scores": 2, "gelu_tanh": 2.1, "gelu_t": 3, "norm_1": 5, "scores": 8,
        "probs": 9.27, "tokens_t": 13.2, "route": 14},
    "gpsimd": {"norm_x": 0, "cross_out": 4, "cross_bias": 4.1, "qkv": 5.79, "project": 11, "norm_2": 12,
        "tokens_t": 13},
    "sync": {"values_copy": 7, "load_w3": 7.5, "weights_copy": 16},
}
SLOT_STRIDE = 2.15
FFN_AFTER_TILE = 17
FFN_START = 16
FFN_PER_SLOT = 2.66
SPLIT_START = 12
SPLITS_PER_SLOT = 2
RING = 4
SPLIT = 2


def bass_perceiver_block(nc, x, ctx_rows, ctx_cols, wqkv, bqkv, head_w, wo, bo, gate_w, rms_w, w12_d, w3,
                         ident, score_bias, batch_head_mask, value_mask, expert_ids, out):
    N, D = x.shape
    NB, S = ctx_cols.shape[1], ctx_cols.shape[2]
    T = N // NB
    BT = P // T
    NT = N // P
    SC = S // P
    NKV = value_mask.shape[1]
    KV = wqkv.shape[1] - D >> 1
    HD = KV // NKV
    QK = D + KV
    E = gate_w.shape[1]
    CHUNKS = w12_d.shape[2] // P
    DE = w12_d.shape[2] // E
    HALF = 2 * P
    TPH = HALF // P
    HALVES = N // HALF
    YW = KV + NKV

    def plan(engine):
        work = [(slot + SLOT_STRIDE * q, 0, q, stage) for stage, slot in STAGE_SLOT[engine].items() for q in range(NT)]
        for i in range(HALVES * CHUNKS):
            last_tile = TPH * (i // CHUNKS + 1) - 1
            slot = max(FFN_START + i / FFN_PER_SLOT, FFN_AFTER_TILE + SLOT_STRIDE * last_tile)
            work.append((slot, 1, i, "expert"))
        for i in range(CHUNKS // SPLIT):
            work.append((SPLIT_START + i / SPLITS_PER_SLOT, 2, i, "split"))
        return [(stage, n) for _, _, n, stage in sorted(work)]

    BANKS = [
        {"cross_scores": "act_done", "scores": "pre_done"},
        {"gelu_t": "actT_done", "probs": "probsT_done"},
        {"latents_t": "xnT0_done", "norm_1": "xnT1_done", "tokens_t": "yT_hi_done"},
        {"cross_out": "x1_done", "qkv": "qk_done", "values": "y_heads_done", "project": "x2_done",
         "route": "logits_copied", "weights_t": "wT_done"},
    ]
    FREED_BY = {}
    for bank in BANKS:
        users = [(stage, q) for stage, q in plan("tensor") if stage in bank]
        for (before, q0), user in zip(users, users[1:]):
            FREED_BY[user] = bank[before], q0 + 1

    with ExitStack() as stack:
        def sb(name, shape, dt=F32):
            return stack.enter_context(nc.sbuf_tensor(name, shape, dt))

        def pb(name):
            return stack.enter_context(nc.psum_tensor(name, [P, 512], F32))

        def sem(name):
            return stack.enter_context(nc.semaphore(name))

        x_sb = sb("x_sb", [P, NT, D])
        ctx_r = sb("ctx_r", [P, NB, SC, D])
        ctx_c = sb("ctx_c", [P, NB, S])
        wqkv_sb = sb("wqkv_sb", [P, QK + KV])
        bqkv_sb = sb("bqkv_sb", [P, QK + KV])
        head_sb = sb("head_sb", [P, QK])
        wo_sb = sb("wo_sb", [P, D])
        bo_sb = sb("bo_sb", [P, D])
        gate_sb = sb("gate_sb", [P, E])
        rms_sb = sb("rms_sb", [P, D])
        w12 = sb("w12", [P, RING, 2, SPLIT * P])
        w_bcast = ctx_c[:, 0:E, :]
        w3_sb = ctx_r[:, 0:2 * BT, :, :].rearrange("p b c d -> p (b c) d")[:, 0:CHUNKS, :]
        ident_sb = sb("ident_sb", [P, P])
        bias_sb = sb("bias_sb", [P, NKV, T])
        bh_mask = sb("bh_mask", [P, BT * NKV])
        v_mask = sb("v_mask", [P, NKV])
        ids_sb = sb("ids_sb", [P, E])
        w12_hi = sb("w12_hi", [P, 2, CHUNKS * P], F32R)
        w12_lo = sb("w12_lo", [P, 2, CHUNKS * P], F32R)

        stats = sb("stats", [P, 3, NT, 6])
        mean_var = sb("mean_var", [P, 3, NT, 2])
        var_eps = sb("var_eps", [P, 3, NT])
        rstd = sb("rstd", [P, 3, NT])
        minus_half = sb("minus_half", [P, D // HD + NKV])
        xn = sb("xn", [P, 3, NT, D])
        xnT = sb("xnT", [P, 3, NT, P])
        gelu_rows = sb("gelu_rows", [P, 2, S])
        actT = sb("actT", [P, 2, SC, P])
        x1 = sb("x1", [P, NT, D])
        qk = sb("qk", [P, NT, QK + KV])
        qk_sq = sb("qk_sq", [P, 2, QK])
        qk_ms = sb("qk_ms", [P, NT, QK // HD])
        qk_rs = sb("qk_rs", [P, NT, QK // HD])
        v_rep = sb("v_rep", [P, NT, BT, KV])
        v_all = sb("v_all", [P, NT, BT, YW])
        qkT = sb("qkT", [P, NT, QK])
        k_blocks = sb("k_blocks", [P, 2, BT * NKV, T])
        pre = sb("pre", [P, 2, BT * NKV, T])
        row_max = sb("row_max", [P, NT, BT * NKV])
        probs = sb("probs", [P, 2, BT * NKV, T])
        probsT = sb("probsT", [P, 2, BT, P])
        inv_sum = sb("inv_sum", [P, NT, BT, NKV])
        y_heads = sb("y_heads", [P, NT, BT, KV])
        yT_heads = sb("yT_heads", [P, NT, P])
        x1b = sb("x1b", [P, NT, D])
        x2 = sb("x2", [P, NT, D])
        rms = sb("rms", [P, NT, 4])
        y_tok = sb("y_tok", [P, NT, D])
        yT = sb("yT", [P, N])
        yT_hi = sb("yT_hi", [P, N], F32R)
        yT_lo = sb("yT_lo", [P, N], F32R)
        resid = sb("resid", [P, NT, D])
        top = sb("top", [P, NT, 8])
        top_id = sb("top_id", [P, NT, 8], U32)
        top_idf = sb("top_idf", [P, NT, 2])
        pick = sb("pick", [P, 5, NT])
        diff, ratio, denom, p_first, p_second = (pick[:, k, :] for k in range(5))
        w_first = sb("w_first", [P, NT, E])
        w_second = sb("w_second", [P, NT, E])
        w_full = sb("w_full", [P, NT, E])
        wT = sb("wT", [E, NT, P])
        logit_sb = sb("logit_sb", [P, NT, E])
        ffn_t = sb("ffn_t", [P, 2, HALF])
        ffn_u = sb("ffn_u", [P, 2, HALF])
        ffn_v = sb("ffn_v", [P, 3, HALF])
        ffn_h = sb("ffn_h", [P, 3, HALF])
        combT = sb("combT", [P, HALVES, HALF])

        row_ps = pb("row_ps")
        wide_ps = pb("wide_ps")
        small_ps = pb("small_ps")
        outs_ps = pb("outs_ps")
        expert_ps = [pb(f"expert_ps{i}") for i in range(3)]
        comb_ps = pb("comb_ps")

        names = """x_in consts_in attn_in ffn_small_in w3_in
            minus_half_set
            stats0_done stats1_done stats2_done mean0_done mean1_done mean2_done var0_done var1_done var2_done
            rstd0_done rstd1_done rstd2_done xn0_done xn1_done xn2_done xnT0_ps xnT1_ps xnT0_done xnT1_done
            h_done sq_done cubic_done th_done act_done actT_ps actT_done cross_done x1_done
            x1b_done head_w_done sums_set qkv_done qk_done qk_sq_done qk_sum_done qk_ms_done qk_rs_done
            v_done qk_scaled qk_ready qkT_done k_blocks_done s_done pre_done max_done centred_done
            probs_done probsT_ps probsT_done y_done inv_done y_heads_done yT_heads_done o_done x2_done
            rms_steps rms_done y_tok_done resid_done yT_ps yT_done yT_hi_done yT_lo_done
            logits_done logits_copied top_done top_id_done top_idf_done diff_done exp_done denom_done
            p1_done p2_done w_first_done w_second_done w_full_done wT_ps wT_done w_stored v_stored
            w_hi_done w_lo_done gates_ps tanh_done u_done expert_read h_piece_done h_whole_done down_done
            combT_done out_ps out_ready stored""".split()
        s = {n: sem(n) for n in names}
        v_rep_in = [sem(f"v_rep_in{q}") for q in range(NT)]
        w_bcast_in = [sem(f"w_bcast_in{q}") for q in range(NT)]
        w12_in = [sem(f"w12_in{n}") for n in range(RING)]
        ctx_in = [sem(f"ctx_in{q}") for q in range(NT)]
        v_dram = nc.dram_tensor("v_dram", (NT, BT, T, KV), F32, kind="Internal").ap()
        w_dram = nc.dram_tensor("w_dram", (NT, E, P), F32, kind="Internal").ap()
        block = stack.enter_context(nc.Block())

        def batches(q):
            return slice(BT * q, BT * q + BT)

        def tile(q):
            return slice(P * q, P * q + P)

        def half(h):
            return slice(HALF * h, HALF * h + HALF)

        def experts_of(c):
            at, found = 0, []
            while at < P:
                e = (c * P + at) // DE
                n = min((e + 1) * DE - c * P, P) - at
                n = min(n, {0: P, 64: 64}.get(at, 32))
                found.append((e, at, n))
                at += n
            return found

        PIECES = []
        for i in range(HALVES * CHUNKS):
            n = len(experts_of(i % CHUNKS))
            whole, pieces = PIECES[-1] if PIECES else (0, 0)
            PIECES.append((whole + 1, pieces) if n == 1 else (whole, pieces + n))

        def h_ready(eng, i):
            whole, pieces = PIECES[i]
            if len(experts_of(i % CHUNKS)) == 1:
                eng.wait_ge(s["h_whole_done"], whole)
            else:
                eng.wait_ge(s["h_piece_done"], pieces)

        @block.sync
        def _(sp):
            sp.dma_start(x_sb[:], x.rearrange("(q p) d -> p q d", p=P)).then_inc(s["x_in"], 16)
            sp.dma_start(ident_sb[:], ident).then_inc(s["consts_in"], 16)
            for q in range(NT):
                sp.dma_start(ctx_c[:, batches(q), :], ctx_cols[:, batches(q), :]).then_inc(ctx_in[q], 16)
                sp.dma_start(ctx_r[:, batches(q), :, :], ctx_rows[:, batches(q), :, :]).then_inc(ctx_in[q], 16)
                if q == 0:
                    sp.dma_start(wqkv_sb[:], wqkv).then_inc(s["attn_in"], 16)
                    sp.dma_start(bqkv_sb[:], bqkv.partition_broadcast(P)).then_inc(s["attn_in"], 16)
                    sp.dma_start(head_sb[:], head_w.partition_broadcast(P)).then_inc(s["attn_in"], 16)
                    sp.dma_start(wo_sb[:], wo).then_inc(s["attn_in"], 16)
                    sp.dma_start(bo_sb[:], bo.partition_broadcast(P)).then_inc(s["attn_in"], 16)
                    sp.dma_start(bias_sb[:], score_bias).then_inc(s["attn_in"], 16)
                    sp.dma_start(bh_mask[:], batch_head_mask).then_inc(s["attn_in"], 16)
                    sp.dma_start(v_mask[:], value_mask).then_inc(s["attn_in"], 16)
                    sp.dma_start(gate_sb[:], gate_w).then_inc(s["ffn_small_in"], 16)
                    sp.dma_start(rms_sb[:], rms_w.partition_broadcast(P)).then_inc(s["ffn_small_in"], 16)
                    sp.dma_start(ids_sb[:], expert_ids.partition_broadcast(P)).then_inc(s["ffn_small_in"], 16)
            def load_w12(n):
                sp.dma_start(w12[:, n % RING, :, :], w12_d[:, :, n * SPLIT * P:(n + 1) * SPLIT * P]).then_inc(w12_in[n % RING], 16)

            for n in range(RING):
                load_w12(n)
            for stage, q in plan("sync"):
                if stage == "values_copy":
                    sp.wait_ge(s["qk_done"], q + 1)
                    sp.dma_start(v_dram[q].rearrange("b t v -> (b t) v"), qk[:, q, QK:QK + KV]).then_inc(s["v_stored"], 16)
                    sp.wait_ge(s["v_stored"], 16 * (q + 1))
                    for g in range(NKV):
                        sp.dma_start(v_rep[T * g:T * g + T, q, :, :],
                                     v_dram[q].rearrange("b t v -> t b v")).then_inc(v_rep_in[q], 16)
                elif stage == "load_w3":
                    if q == 0:
                        sp.wait_ge(s["cross_done"], 2)
                        sp.dma_start(w3_sb, w3).then_inc(s["w3_in"], 16)
                elif stage == "split" and q + RING < CHUNKS // SPLIT:
                    sp.wait_ge(s["w_lo_done"], q + 1)
                    load_w12(q + RING)
                elif stage == "weights_copy":
                    sp.wait_ge(s["wT_done"], q + 1)
                    sp.dma_start(w_dram[q], wT[:, q, :]).then_inc(s["w_stored"], 16)
                    sp.wait_ge(s["w_stored"], 16 * (q + 1))
                    sp.wait_ge(s["h_done"], 2)
                    sp.dma_start(w_bcast[:, :, tile(q)], w_dram[q].partition_broadcast(P)).then_inc(w_bcast_in[q], 16)
            out_v = out.rearrange("(q p) d -> q p d", p=P)
            for q in range(NT):
                sp.wait_ge(s["out_ready"], q + 1)
                sp.dma_start(out_v[q], resid[:, q, :]).then_inc(s["stored"], 16)
            sp.wait_ge(s["stored"], 16 * NT)

        ATTN_IN, FFN_SMALL_IN = 16 * 8, 16 * 3

        @block.tensor
        def _(pe):
            pe.wait_ge(s["consts_in"], 16)

            def bank_free(stage, q):
                if (stage, q) in FREED_BY:
                    signal, count = FREED_BY[stage, q]
                    pe.wait_ge(s[signal], count)

            def transpose_rows(q, src, src_ready, done, stage):
                pe.wait_ge(src_ready, q + 1)
                bank_free(stage, q)
                pe.transpose(small_ps[:, 0:P], src, ident_sb[:]).then_inc(done, 1)

            def down(i):
                h, c = divmod(i, CHUNKS)
                h_ready(pe, i)
                if i == 0:
                    pe.wait_ge(s["w3_in"], 16)
                if c == 0 and h:
                    pe.wait_ge(s["combT_done"], h)
                pe.matmul(comb_ps[:, 0:HALF], w3_sb[:, c, :], ffn_h[:, i % 3, :],
                          start=(c == 0), stop=(c == CHUNKS - 1)).then_inc(s["down_done"], 1)

            for stage, q in plan("tensor"):
                if stage == "latents_t":
                    transpose_rows(q, xn[:, 0, q, :], s["xn0_done"], s["xnT0_ps"], stage)
                elif stage == "cross_scores":
                    pe.wait_ge(s["xnT0_done"], q + 1)
                    pe.wait_ge(ctx_in[q], 32)
                    bank_free(stage, q)
                    for j in range(BT):
                        mm = pe.matmul(row_ps[T * j:T * j + T, 0:S], xnT[:, 0, q, T * j:T * j + T],
                                       ctx_c[:, BT * q + j, :], start=True, stop=True)
                    mm.then_inc(s["h_done"], 1)
                elif stage == "gelu_t":
                    pe.wait_ge(s["act_done"], q + 1)
                    bank_free(stage, q)
                    for c in range(SC):
                        mm = pe.transpose(wide_ps[:, c * P:c * P + P], gelu_rows[:, q % 2, c * P:c * P + P], ident_sb[:])
                    mm.then_inc(s["actT_ps"], 1)
                elif stage == "cross_out":
                    pe.wait_ge(s["actT_done"], q + 1)
                    bank_free(stage, q)
                    for c in range(SC):
                        for j in range(BT):
                            mm = pe.matmul(outs_ps[T * j:T * j + T, 0:D], actT[:, q % 2, c, T * j:T * j + T],
                                           ctx_r[:, BT * q + j, c, :], start=(c == 0), stop=(c == SC - 1),
                                           skip_group_check=True)
                    mm.then_inc(s["cross_done"], 1)
                elif stage == "norm_1":
                    transpose_rows(q, xn[:, 1, q, :], s["xn1_done"], s["xnT1_ps"], stage)
                elif stage == "qkv":
                    pe.wait_ge(s["xnT1_done"], q + 1)
                    pe.wait_ge(s["attn_in"], ATTN_IN)
                    bank_free(stage, q)
                    pe.matmul(outs_ps[:, 0:QK + KV], xnT[:, 1, q, :], wqkv_sb[:], start=True,
                              stop=True).then_inc(s["qkv_done"], 1)
                elif stage == "scores":
                    pe.wait_ge(s["k_blocks_done"], q + 1)
                    bank_free(stage, q)
                    pe.matmul(row_ps[:, :], qkT[:, q, 0:D], k_blocks[:, q % 2, :, :].rearrange("p a t -> p (a t)"),
                              start=True, stop=True).then_inc(s["s_done"], 1)
                elif stage == "probs":
                    pe.wait_ge(s["probs_done"], q + 1)
                    bank_free(stage, q)
                    for j in range(BT):
                        rows = probs[:, q % 2, NKV * j:NKV * j + NKV, :].rearrange("p a t -> p (a t)")
                        mm = pe.transpose(wide_ps[:, P * j:P * j + P], rows, ident_sb[:])
                    mm.then_inc(s["probsT_ps"], 1)
                elif stage == "values":
                    pe.wait_ge(s["probsT_done"], q + 1)
                    pe.wait_ge(s["v_done"], q + 1)
                    bank_free(stage, q)
                    for j in range(BT):
                        mm = pe.matmul(outs_ps[:, YW * j:YW * j + YW], probsT[:, q % 2, j, :], v_all[:, q, j, :],
                                       start=True, stop=True)
                    mm.then_inc(s["y_done"], 1)
                elif stage == "project":
                    pe.wait_ge(s["yT_heads_done"], q + 1)
                    bank_free(stage, q)
                    pe.matmul(outs_ps[:, 0:D], yT_heads[:, q, :], wo_sb[:], start=True, stop=True).then_inc(s["o_done"], 1)
                elif stage == "tokens_t":
                    transpose_rows(q, y_tok[:, q, :], s["y_tok_done"], s["yT_ps"], stage)
                elif stage == "route":
                    pe.wait_ge(s["yT_done"], q + 1)
                    pe.wait_ge(s["ffn_small_in"], FFN_SMALL_IN)
                    bank_free(stage, q)
                    pe.matmul(outs_ps[:, 0:E], yT[:, tile(q)], gate_sb[:], start=True, stop=True).then_inc(s["logits_done"], 1)
                elif stage == "weights_t":
                    pe.wait_ge(s["w_full_done"], q + 1)
                    bank_free(stage, q)
                    pe.transpose(outs_ps[0:E, 0:P], w_full[:, q, :], ident_sb[:]).then_inc(s["wT_ps"], 1)
                elif stage == "expert":
                    i = q
                    h, c = divmod(i, CHUNKS)
                    if c == 0:
                        pe.wait_ge(s["yT_hi_done"], TPH * (h + 1))
                        pe.wait_ge(s["yT_lo_done"], TPH * (h + 1))
                    if h == 0:
                        pe.wait_ge(s["w_lo_done"], c // SPLIT + 1)
                    if i >= 3:
                        pe.wait_ge(s["expert_read"], i - 2)
                    cols = slice(c * P, c * P + P)
                    for k in range(2):
                        o = expert_ps[i % 3][:, HALF * k:HALF * k + HALF]
                        pe.matmul(o, w12_hi[:, k, cols], yT_hi[:, half(h)], start=True, stop=False)
                        pe.matmul(o, w12_hi[:, k, cols], yT_lo[:, half(h)], start=False, stop=False)
                        mm = pe.matmul(o, w12_lo[:, k, cols], yT_hi[:, half(h)], start=False, stop=True)
                    mm.then_inc(s["gates_ps"], 1)
                    if i >= 2:
                        down(i - 2)
            for i in range(HALVES * CHUNKS - 2, HALVES * CHUNKS):
                down(i)
            for q in range(NT):
                pe.wait_ge(s["combT_done"], q // TPH + 1)
                bank = expert_ps[q % 3]
                if q >= 3:
                    pe.wait_ge(s["out_ready"], q - 2)
                else:
                    pe.wait_ge(s["expert_read"], HALVES * CHUNKS)
                pe.transpose(bank[:, 0:P], combT[:, q // TPH, P * (q % TPH):P * (q % TPH) + P],
                             ident_sb[:]).then_inc(s["out_ps"], 1)

        @block.scalar
        def _(act):
            for stage, q in plan("scalar"):
                if stage == "latents_t":
                    act.wait_ge(s["xnT0_ps"], q + 1)
                    act.activation(xnT[:, 0, q, :], small_ps[:, 0:P], ACT.Copy).then_inc(s["xnT0_done"], 1)
                elif stage == "cross_scores":
                    act.wait_ge(s["h_done"], q + 1)
                    if q >= 2:
                        act.wait_ge(s["actT_ps"], q - 1)
                    act.activation(gelu_rows[:, q % 2, :], row_ps[:, :], ACT.Square).then_inc(s["sq_done"], 1)
                elif stage == "gelu_tanh":
                    act.wait_ge(s["cubic_done"], q + 1)
                    act.activation(gelu_rows[:, q % 2, :], gelu_rows[:, q % 2, :], ACT.Tanh,
                                   scale=GELU_SCALE * GELU_CUBIC).then_inc(s["th_done"], 1)
                elif stage == "gelu_t":
                    act.wait_ge(s["actT_ps"], q + 1)
                    if q >= 2:
                        act.wait_ge(s["cross_done"], q - 1)
                    act.activation(actT[:, q % 2, :, :].rearrange("p c t -> p (c t)"), wide_ps[:, :],
                                   ACT.Copy).then_inc(s["actT_done"], 1)
                elif stage == "norm_1":
                    act.wait_ge(s["xnT1_ps"], q + 1)
                    act.activation(xnT[:, 1, q, :], small_ps[:, 0:P], ACT.Copy).then_inc(s["xnT1_done"], 1)
                elif stage == "scores":
                    act.wait_ge(s["centred_done"], q + 1)
                    if q >= 2:
                        act.wait_ge(s["probsT_ps"], q - 1)
                    act.activation(probs[:, q % 2, :, :], pre[:, q % 2, :, :], ACT.Exp).then_inc(s["probs_done"], 1)
                elif stage == "probs":
                    act.wait_ge(s["probsT_ps"], q + 1)
                    if q >= 2:
                        act.wait_ge(s["y_done"], q - 1)
                    act.activation(probsT[:, q % 2, :, :].rearrange("p c t -> p (c t)"), wide_ps[:, :],
                                   ACT.Copy).then_inc(s["probsT_done"], 1)
                elif stage == "tokens_t":
                    act.wait_ge(s["yT_ps"], q + 1)
                    act.activation(yT[:, tile(q)], small_ps[:, 0:P], ACT.Copy).then_inc(s["yT_done"], 1)
                    act.activation(yT_hi[:, tile(q)], small_ps[:, 0:P], ACT.Copy).then_inc(s["yT_hi_done"], 1)
                elif stage == "route":
                    act.wait_ge(s["diff_done"], q + 1)
                    act.activation(ratio[:, q:q + 1], diff[:, q:q + 1], ACT.Exp).then_inc(s["exp_done"], 1)
                elif stage == "split":
                    cols = slice(q * SPLIT * P, (q + 1) * SPLIT * P)
                    act.wait_ge(w12_in[q % RING], 16 * (q // RING + 1))
                    act.activation(w12_hi[:, :, cols], w12[:, q % RING, :, :], ACT.Copy).then_inc(s["w_hi_done"], 1)
                elif stage == "expert":
                    i = q
                    act.wait_ge(s["gates_ps"], i + 1)
                    if i >= 2:
                        act.wait_ge(s["u_done"], i - 1)
                    act.activation(ffn_t[:, i % 2, :], expert_ps[i % 3][:, 0:HALF], ACT.Tanh,
                                   scale=0.5).then_inc(s["tanh_done"], 1)
                    h, c = divmod(i, CHUNKS)
                    if h and c == 1:
                        act.wait_ge(s["down_done"], CHUNKS * h)
                        act.activation(combT[:, h - 1, :], comb_ps[:, 0:HALF], ACT.Copy, scale=0.5).then_inc(s["combT_done"], 1)
            act.wait_ge(s["down_done"], CHUNKS * HALVES)
            act.activation(combT[:, HALVES - 1, :], comb_ps[:, 0:HALF], ACT.Copy, scale=0.5).then_inc(s["combT_done"], 1)

        @block.gpsimd
        def _(pool):
            pool.memset(minus_half[:], -0.5).then_inc(s["minus_half_set"], 1)
            pool.wait_ge(s["minus_half_set"], 1)

            def rsqrt_var(k, q):
                pool.wait_ge(s[f"var{k}_done"], q + 1)
                pool.tensor_tensor(rstd[:, k, q:q + 1], var_eps[:, k, q:q + 1], minus_half[:, 0:1],
                                   ALU.pow).then_inc(s[f"rstd{k}_done"], 1)

            for stage, q in plan("gpsimd"):
                if stage == "norm_x":
                    rsqrt_var(0, q)
                elif stage == "cross_out":
                    rsqrt_var(1, q)
                elif stage == "cross_bias":
                    pool.wait_ge(s["x1_done"], q + 1)
                    pool.wait_ge(s["attn_in"], ATTN_IN)
                    pool.tensor_tensor(x1b[:, q, :], x1[:, q, :], bo_sb[:], ALU.add).then_inc(s["x1b_done"], 1)
                elif stage == "qkv":
                    pool.wait_ge(s["qk_ms_done"], q + 1)
                    pool.tensor_tensor(qk_rs[:, q, :], qk_ms[:, q, :], minus_half[:, 0:QK // HD],
                                       ALU.pow).then_inc(s["qk_rs_done"], 1)
                elif stage == "project":
                    rsqrt_var(2, q)
                    r, v, m = rstd[:, 2, q:q + 1], mean_var[:, 2, q, 1:2], [rms[:, q, k:k + 1] for k in range(4)]
                    pool.wait_ge(s["rstd2_done"], q + 1)
                    pool.tensor_tensor(m[0], r, r, ALU.mult).then_inc(s["rms_steps"], 1)
                    pool.wait_ge(s["rms_steps"], 3 * q + 1)
                    pool.tensor_tensor(m[1], m[0], v, ALU.mult).then_inc(s["rms_steps"], 1)
                    pool.wait_ge(s["rms_steps"], 3 * q + 2)
                    pool.tensor_scalar(m[2], m[1], RMS_EPS, None, ALU.add).then_inc(s["rms_steps"], 1)
                    pool.wait_ge(s["rms_steps"], 3 * q + 3)
                    pool.tensor_tensor(m[3], m[2], minus_half[:, 0:1], ALU.pow).then_inc(s["rms_done"], 1)
                elif stage == "norm_2":
                    pool.wait_ge(s["xn2_done"], q + 1)
                    pool.tensor_tensor(resid[:, q, :], x2[:, q, :], xn[:, 2, q, :], ALU.add).then_inc(s["resid_done"], 1)
                elif stage == "tokens_t":
                    pool.wait_ge(s["yT_hi_done"], q + 1)
                    pool.tensor_tensor(yT_lo[:, tile(q)], yT[:, tile(q)], yT_hi[:, tile(q)].bitcast(F32),
                                       ALU.subtract).then_inc(s["yT_lo_done"], 1)
                elif stage == "expert":
                    i = q
                    h, c = divmod(i, CHUNKS)
                    if len(experts_of(c)) > 1:
                        continue
                    pool.wait_ge(s["expert_read"], i + 1)
                    if c == 0:
                        for t in range(TPH * h, TPH * (h + 1)):
                            pool.wait_ge(w_bcast_in[t], 16)
                    if i >= 3:
                        pool.wait_ge(s["down_done"], i - 2)
                    (e, _, _), = experts_of(c)
                    pool.tensor_tensor(ffn_h[:, i % 3, :], ffn_v[:, i % 3, :], w_bcast[:, e, half(h)],
                                       ALU.mult).then_inc(s["h_whole_done"], 1)

        @block.vector
        def _(dve):
            def row_stats(k, q, src):
                dve.bn_stats(stats[:, k, q, :], src).then_inc(s[f"stats{k}_done"], 1)
                dve.wait_ge(s[f"stats{k}_done"], q + 1)
                dve.bn_aggr(mean_var[:, k, q, :], stats[:, k, q, :]).then_inc(s[f"mean{k}_done"], 1)
                dve.wait_ge(s[f"mean{k}_done"], q + 1)
                dve.tensor_scalar(var_eps[:, k, q:q + 1], mean_var[:, k, q, 1:2], LN_EPS, None,
                                  ALU.add).then_inc(s[f"var{k}_done"], 1)

            def normalise(k, q, src):
                dve.wait_ge(s[f"rstd{k}_done"], q + 1)
                dve.tensor_scalar(xn[:, k, q, :], src, mean_var[:, k, q, 0:1], rstd[:, k, q:q + 1],
                                  ALU.subtract, ALU.mult).then_inc(s[f"xn{k}_done"], 1)

            dve.wait_ge(s["x_in"], 16)
            for stage, q in plan("vector"):
                if stage == "norm_x":
                    row_stats(0, q, x_sb[:, q, :])
                elif stage == "latents_t":
                    normalise(0, q, x_sb[:, q, :])
                elif stage == "cross_scores":
                    dve.wait_ge(s["sq_done"], q + 1)
                    dve.scalar_tensor_tensor(out=gelu_rows[:, q % 2, :], in0=gelu_rows[:, q % 2, :], scalar=1.0 / GELU_CUBIC,
                                             in1=row_ps[:, :], op0=ALU.add, op1=ALU.mult).then_inc(s["cubic_done"], 1)
                elif stage == "gelu_t":
                    dve.wait_ge(s["th_done"], q + 1)
                    dve.scalar_tensor_tensor(out=gelu_rows[:, q % 2, :], in0=gelu_rows[:, q % 2, :], scalar=1.0,
                                             in1=row_ps[:, :], op0=ALU.add,
                                             op1=ALU.mult).then_inc(s["act_done"], 1)
                elif stage == "cross_out":
                    dve.wait_ge(s["cross_done"], q + 1)
                    dve.scalar_tensor_tensor(out=x1[:, q, :], in0=outs_ps[:, 0:D], scalar=0.5, in1=x_sb[:, q, :],
                                             op0=ALU.mult, op1=ALU.add).then_inc(s["x1_done"], 1)
                    dve.wait_ge(s["x1_done"], q + 1)
                    row_stats(1, q, x1[:, q, :])
                elif stage == "norm_1":
                    normalise(1, q, x1[:, q, :])
                elif stage == "qkv":
                    if q == 0:
                        dve.wait_ge(s["attn_in"], ATTN_IN)
                        dve.tensor_scalar(head_sb[:, 0:D], head_sb[:, 0:D], float(HD) ** -0.5, None,
                                          ALU.mult).then_inc(s["head_w_done"], 1)
                        dve.tensor_copy(v_all[:, :, :, KV:YW].rearrange("p q b g -> p (q b) g"),
                                        v_mask[:].unsqueeze(1).broadcast_to([P, NT * BT, NKV])).then_inc(s["sums_set"], 1)
                    dve.wait_ge(s["qkv_done"], q + 1)
                    dve.tensor_tensor(qk[:, q, :], outs_ps[:, 0:QK + KV], bqkv_sb[:], ALU.add).then_inc(s["qk_done"], 1)
                    dve.wait_ge(s["qk_done"], q + 1)
                    dve.tensor_tensor(qk_sq[:, q % 2, :], qk[:, q, 0:QK], qk[:, q, 0:QK], ALU.mult).then_inc(s["qk_sq_done"], 1)
                    dve.wait_ge(s["qk_sq_done"], q + 1)
                    dve.tensor_reduce(qk_ms[:, q, :], qk_sq[:, q % 2, :].rearrange("p (h d) -> p h d", d=HD),
                                      AX_X, ALU.add).then_inc(s["qk_sum_done"], 1)
                    dve.wait_ge(s["qk_sum_done"], q + 1)
                    dve.tensor_scalar(qk_ms[:, q, :], qk_ms[:, q, :], 1.0 / HD, QK_EPS, ALU.mult,
                                      ALU.add).then_inc(s["qk_ms_done"], 1)
                elif stage == "head_norm":
                    dve.wait_ge(s["qk_rs_done"], q + 1)
                    dve.wait_ge(s["head_w_done"], 1)
                    heads = qk[:, q, 0:QK].rearrange("p (h d) -> p h d", d=HD)
                    dve.tensor_tensor(heads, heads, qk_rs[:, q, :].unsqueeze(2).broadcast_to([P, QK // HD, HD]),
                                      ALU.mult).then_inc(s["qk_scaled"], 1)
                    dve.wait_ge(s["qk_scaled"], q + 1)
                    dve.tensor_tensor(qk[:, q, 0:QK], qk[:, q, 0:QK], head_sb[:], ALU.mult).then_inc(s["qk_ready"], 1)
                    dve.wait_ge(s["qk_ready"], q + 1)
                    dve.transpose(qkT[:, q, :], qk[:, q, 0:QK]).then_inc(s["qkT_done"], 1)
                    dve.wait_ge(s["qkT_done"], q + 1)
                    if q >= 2:
                        dve.wait_ge(s["s_done"], q - 1)
                    dve.tensor_tensor(k_blocks[:, q % 2, :, :],
                                      qkT[:, q, D:QK].unsqueeze(1).broadcast_to([P, BT * NKV, T]),
                                      bh_mask[:].unsqueeze(2).broadcast_to([P, BT * NKV, T]),
                                      ALU.mult).then_inc(s["k_blocks_done"], 1)
                elif stage == "scores":
                    dve.wait_ge(s["s_done"], q + 1)
                    if q >= 2:
                        dve.wait_ge(s["probs_done"], q - 1)
                    flat = pre[:, q % 2, :, :].rearrange("p (b g) t -> p b (g t)", g=NKV)
                    dve.tensor_tensor(flat, row_ps[:, :].rearrange("p (b n) -> p b n", b=BT),
                                      bias_sb[:].rearrange("p g t -> p (g t)").unsqueeze(1).broadcast_to([P, BT, NKV * T]),
                                      ALU.add).then_inc(s["pre_done"], 1)
                    dve.wait_ge(s["pre_done"], q + 1)
                    dve.tensor_reduce(row_max[:, q, :], pre[:, q % 2, :, :], AX_X, ALU.max).then_inc(s["max_done"], 1)
                    dve.wait_ge(s["max_done"], q + 1)
                    dve.tensor_tensor(pre[:, q % 2, :, :], pre[:, q % 2, :, :],
                                      row_max[:, q, :].unsqueeze(2).broadcast_to([P, BT * NKV, T]),
                                      ALU.subtract).then_inc(s["centred_done"], 1)
                elif stage == "value_rows":
                    dve.wait_ge(v_rep_in[q], 16 * NKV)
                    dve.wait_ge(s["sums_set"], 1)
                    dve.tensor_tensor(v_all[:, q, :, 0:KV].rearrange("p b (g d) -> p b g d", g=NKV),
                                      v_rep[:, q, :, :].rearrange("p b (g d) -> p b g d", g=NKV),
                                      v_mask[:].unsqueeze(1).unsqueeze(3).broadcast_to([P, BT, NKV, HD]),
                                      ALU.mult).then_inc(s["v_done"], 1)
                elif stage == "values":
                    y = outs_ps[:, 0:BT * YW].rearrange("p (b n) -> p b n", n=YW)
                    dve.wait_ge(s["y_done"], q + 1)
                    dve.reciprocal(inv_sum[:, q, :, :], y[:, :, KV:YW]).then_inc(s["inv_done"], 1)
                    dve.wait_ge(s["inv_done"], q + 1)
                    dve.tensor_tensor(y_heads[:, q, :, :].rearrange("p b (g d) -> p b g d", g=NKV),
                                      y[:, :, 0:KV].rearrange("p b (g d) -> p b g d", g=NKV),
                                      inv_sum[:, q, :, :].unsqueeze(3).broadcast_to([P, BT, NKV, HD]),
                                      ALU.mult).then_inc(s["y_heads_done"], 1)
                    dve.wait_ge(s["y_heads_done"], q + 1)
                    dve.transpose(yT_heads[:, q, :], y_heads[:, q, :, :].rearrange("p b v -> p (b v)")).then_inc(s["yT_heads_done"], 1)
                elif stage == "project":
                    dve.wait_ge(s["o_done"], q + 1)
                    dve.wait_ge(s["x1b_done"], q + 1)
                    dve.tensor_tensor(x2[:, q, :], outs_ps[:, 0:D], x1b[:, q, :], ALU.add).then_inc(s["x2_done"], 1)
                    dve.wait_ge(s["x2_done"], q + 1)
                    row_stats(2, q, x2[:, q, :])
                elif stage == "norm_2":
                    normalise(2, q, x2[:, q, :])
                    dve.wait_ge(s["xn2_done"], q + 1)
                    dve.wait_ge(s["rms_done"], q + 1)
                    dve.wait_ge(s["ffn_small_in"], FFN_SMALL_IN)
                    dve.scalar_tensor_tensor(out=y_tok[:, q, :], in0=xn[:, 2, q, :], scalar=rms[:, q, 3:4],
                                             in1=rms_sb[:], op0=ALU.mult, op1=ALU.mult).then_inc(s["y_tok_done"], 1)
                elif stage == "route":
                    one = slice(q, q + 1)
                    dve.wait_ge(s["logits_done"], q + 1)
                    dve.tensor_copy(logit_sb[:, q, :], outs_ps[:, 0:E]).then_inc(s["logits_copied"], 1)
                    dve.wait_ge(s["logits_copied"], q + 1)
                    dve.max(top[:, q, :], logit_sb[:, q, :]).then_inc(s["top_done"], 1)
                    dve.wait_ge(s["top_done"], q + 1)
                    dve.tensor_tensor(diff[:, one], top[:, q, 1:2], top[:, q, 0:1], ALU.subtract).then_inc(s["diff_done"], 1)
                    dve.max_index(top_id[:, q, :], top[:, q, :], logit_sb[:, q, :]).then_inc(s["top_id_done"], 1)
                    dve.wait_ge(s["top_id_done"], q + 1)
                    dve.tensor_copy(top_idf[:, q, :], top_id[:, q, 0:2]).then_inc(s["top_idf_done"], 1)
                elif stage == "route_weights":
                    one = slice(q, q + 1)
                    dve.wait_ge(s["exp_done"], q + 1)
                    dve.tensor_scalar(denom[:, one], ratio[:, one], 1.0, None, ALU.add).then_inc(s["denom_done"], 1)
                    dve.wait_ge(s["denom_done"], q + 1)
                    dve.reciprocal(p_first[:, one], denom[:, one]).then_inc(s["p1_done"], 1)
                    dve.wait_ge(s["p1_done"], q + 1)
                    dve.tensor_tensor(p_second[:, one], ratio[:, one], p_first[:, one], ALU.mult).then_inc(s["p2_done"], 1)
                    dve.wait_ge(s["top_idf_done"], q + 1)
                    dve.tensor_scalar(w_first[:, q, :], ids_sb[:], top_idf[:, q, 0:1], p_first[:, one],
                                      ALU.is_equal, ALU.mult).then_inc(s["w_first_done"], 1)
                    dve.wait_ge(s["p2_done"], q + 1)
                    dve.tensor_scalar(w_second[:, q, :], ids_sb[:], top_idf[:, q, 1:2], p_second[:, one],
                                      ALU.is_equal, ALU.mult).then_inc(s["w_second_done"], 1)
                    dve.wait_ge(s["w_first_done"], q + 1)
                    dve.wait_ge(s["w_second_done"], q + 1)
                    dve.tensor_tensor(w_full[:, q, :], w_first[:, q, :], w_second[:, q, :], ALU.add).then_inc(s["w_full_done"], 1)
                elif stage == "weights_t":
                    dve.wait_ge(s["wT_ps"], q + 1)
                    dve.tensor_copy(wT[:, q, :], outs_ps[0:E, 0:P]).then_inc(s["wT_done"], 1)
                elif stage == "split":
                    cols = slice(q * SPLIT * P, (q + 1) * SPLIT * P)
                    dve.wait_ge(s["w_hi_done"], q + 1)
                    dve.tensor_tensor(w12_lo[:, :, cols], w12[:, q % RING, :, :], w12_hi[:, :, cols].bitcast(F32),
                                       ALU.subtract).then_inc(s["w_lo_done"], 1)
                elif stage == "expert":
                    i = q
                    up, gate = expert_ps[i % 3][:, 0:HALF], expert_ps[i % 3][:, HALF:2 * HALF]
                    dve.wait_ge(s["tanh_done"], i + 1)
                    dve.scalar_tensor_tensor(out=ffn_u[:, i % 2, :], in0=ffn_t[:, i % 2, :], scalar=1.0, in1=up,
                                             op0=ALU.add, op1=ALU.mult).then_inc(s["u_done"], 1)
                    dve.wait_ge(s["u_done"], i + 1)
                    if i >= 3:
                        h_ready(dve, i - 3)
                    dve.tensor_tensor(ffn_v[:, i % 3, :], ffn_u[:, i % 2, :], gate, ALU.mult).then_inc(s["expert_read"], 1)
                    h, c = divmod(i, CHUNKS)
                    if len(experts_of(c)) > 1:
                        dve.wait_ge(s["expert_read"], i + 1)
                        for t in range(TPH * h, TPH * (h + 1)):
                            dve.wait_ge(w_bcast_in[t], 16)
                        if i >= 3:
                            dve.wait_ge(s["down_done"], i - 2)
                        for e, at, n in experts_of(c):
                            rows = slice(at, at + n)
                            dve.tensor_tensor(ffn_h[rows, i % 3, :], ffn_v[rows, i % 3, :],
                                              w_bcast[rows, e, half(h)], ALU.mult).then_inc(s["h_piece_done"], 1)
            for q in range(NT):
                dve.wait_ge(s["out_ps"], q + 1)
                dve.wait_ge(s["resid_done"], q + 1)
                dve.tensor_tensor(resid[:, q, :], resid[:, q, :], expert_ps[q % 3][:, 0:P], ALU.add).then_inc(s["out_ready"], 1)


def kernel(x, ctx_1024, L0_attn_wq, L0_attn_bq, L0_attn_wkv, L0_attn_bkv, L0_attn_wo, L0_attn_bo,
           L0_attn_qn_w, L0_attn_kn_w, L0_ffn_gate_w, L0_ffn_rms_w, L0_ffn_W1, L0_ffn_W2, L0_ffn_W3):
    import numpy as np
    import concourse.bacc as bacc
    from concourse.bass_utils import run_bass_kernel_spmd

    x, ctx = np.asarray(x), np.asarray(ctx_1024)
    NB, T, D = x.shape
    S = ctx.shape[1]
    HD = L0_attn_qn_w.shape[0]
    H = D // HD
    KV = L0_attn_wkv.shape[1] // 2
    NKV = KV // HD
    REP = H // NKV
    E, DE = L0_ffn_W1.shape[:2]
    BT = P // T
    f32 = np.float32

    def grouped(a):
        a = np.asarray(a)
        return a.reshape(a.shape[:-1] + (NKV, REP, HD)).swapaxes(-3, -2).reshape(a.shape)

    part = np.arange(P)
    slopes = (2.0 ** (-(np.arange(H, dtype=f32) / f32(H - 1) * f32(8.0)))).astype(f32)
    head = np.arange(NKV)[None, :] * REP + (part // T)[:, None]
    dist = ((part % T)[:, None] - np.arange(T)[None, :])[:, None, :]
    score_bias = np.where(dist < 0, f32(-1e30), -slopes[head][:, :, None] * np.abs(dist).astype(f32)).astype(f32)
    batch_head_mask = ((part // HD)[:, None] == np.arange(BT * NKV)[None, :]).astype(f32)
    value_mask = ((part // T)[:, None] == np.arange(NKV)[None, :]).astype(f32)

    arrays = {
        "x": x.reshape(NB * T, D),
        "ctx_rows": ctx.reshape(NB, S // P, P, D).transpose(2, 0, 1, 3),
        "ctx_cols": ctx.transpose(2, 0, 1),
        "wqkv": np.concatenate([grouped(L0_attn_wq), np.asarray(L0_attn_wkv)], axis=1),
        "bqkv": np.concatenate([grouped(L0_attn_bq), np.asarray(L0_attn_bkv)]),
        "head_w": np.concatenate([np.tile(np.asarray(L0_attn_qn_w), H), np.tile(np.asarray(L0_attn_kn_w), NKV)]),
        "wo": np.ascontiguousarray(grouped(np.asarray(L0_attn_wo).T).T),
        "bo": np.asarray(L0_attn_bo),
        "gate_w": np.asarray(L0_ffn_gate_w).T,
        "rms_w": np.asarray(L0_ffn_rms_w),
        "w12": np.stack([np.asarray(w).reshape(E * DE, D).T for w in (L0_ffn_W1, L0_ffn_W2)], axis=1),
        "w3": np.asarray(L0_ffn_W3).transpose(0, 2, 1).reshape(E * DE // P, P, D).transpose(1, 0, 2),
        "ident": np.eye(P, dtype=f32),
        "score_bias": score_bias,
        "batch_head_mask": batch_head_mask,
        "value_mask": value_mask,
        "expert_ids": np.arange(E, dtype=f32),
    }
    arrays = {f"in_{n}": np.ascontiguousarray(a) for n, a in arrays.items()}
    nc = bacc.Bacc("TRN2", target_bir_lowering=False, num_devices=1)
    args = [nc.dram_tensor(n, a.shape, F32, kind="ExternalInput").ap() for n, a in arrays.items()]
    args.append(nc.dram_tensor("out_0", (NB * T, D), F32, kind="ExternalOutput").ap())
    bass_perceiver_block(nc, *args)
    r = run_bass_kernel_spmd(nc, [arrays], core_ids=[0])
    return r.results[0]["out_0"].reshape(NB, T, D)
```

```python
from contextlib import ExitStack

import concourse.bass as bass
from concourse import mybir

F32 = mybir.dt.float32
F32R = mybir.dt.float32r
U32 = mybir.dt.uint32
ALU = mybir.AluOpType
ACT = mybir.ActivationFunctionType
AX_X = mybir.AxisListType.X

P = 128
LN_EPS, QK_EPS, RMS_EPS = 1e-5, 1e-8, 1e-6
GELU_CUBIC = 0.044715
GELU_SCALE = 0.7978845608028654

TIMETABLE = {
    "tensor": {
        "latents_t": (-39, -37, -33, -32), "cross_scores": (-38, -35, -29, -21), "gelu_t": (-36, -31, -26, -17),
        "cross_out": (-34, -27, -25, -15), "norm_1": (-30, -24, -20, -8), "qkv": (-28, -23, -18, -7),
        "scores": (-22, -16, -11, 0.01), "probs": (-19, -13, -3, 3.01), "values": (-14, -12, -1, 5.01),
        "project": (-10, -9, 6.01, 8.01), "tokens_t": (-6, -4, 16.02, 19.02), "route": (-5, -2, 17.02, 19.05),
        "weights_t": (2.01, 7.01, 24.01, 31.01),
        "down": (15.01, 16.01, 17.01, 18.01, 19.01, 19.03, 19.04, 20.01, 21.01, 22.01, 23.01, 25.01, 27.01, 28.01,
            28.02, 29.01, 31.02, 33.01, 34.01, 36.01, 36.02, 36.03, 39.01, 39.02, 40.02, 41.01, 41.02, 41.03, 41.04,
            41.05, 41.06, 41.07, 41.08, 42.01, 42.02, 42.03, 43.01, 43.02, 43.03, 43.04, 43.05, 43.06, 43.07, 43.08),
        "out_t": (40.01, 43.09),
    },
    "vector": {
        "stats_0": (-98, -96, -95, -94), "mean_0": (-97, -92, -89, -88), "norm_0": (-93, -91, -86, -85),
        "gelu_cubic": (-90, -83, -75, -56), "attn_constants": (-87,), "gelu": (-84, -79, -74, -54),
        "cross_residual": (-82, -73, -66, -44), "stats_1": (-81, -72, -64, -42), "mean_1": (-80, -71, -63, -38),
        "norm_1": (-78, -68, -57, -28), "qkv_bias": (-77, -62, -50, -21), "qk_sum": (-76, -61, -48, -18),
        "head_scale": (-70, -55, -39, -12), "head_weights": (-69, -53, -37, -10), "heads_t": (-67, -52, -36, -7),
        "key_blocks": (-65, -51, -35, -5), "score_bias": (-60, -46, -22, 0.01), "score_max": (-59, -45, -19, 0.02),
        "score_centre": (-58, -43, -15, 0.03), "value_rows": (-49, -47, -31, -3),
        "sums_inverse": (-41, -33, -4, 4.01), "value_scale": (-40, -32, -2, 4.02), "values_t": (-34, -30, 3.01, 5.02),
        "attn_residual": (-29, -25, 5.01, 7.02), "stats_2": (-27, -24, 6.01, 9.01), "mean_2": (-26, -23, 7.01, 10.01),
        "norm_2": (-20, -16, 12.01, 16.02), "token_scale": (-17, -14, 13.01, 17.01),
        "top_two": (-13, -11, 16.01, 18.01), "top_difference": (-9, -6, 17.03, 24.01),
        "top_index": (-8, -1, 17.02, 18.02),
        "weigh": (24.02, 27.01, 28.01, 30.01, 34.01, 36.01, 36.02, 39.01, 39.02, 39.03, 39.04, 39.06, 40.01, 41.01,
            42.01, 43.01),
        "output": (39.05, 43.02),
    },
    "scalar": {
        "latents_t": (-43, -42, -36, -35), "gelu_square": (-41, -38, -32, -23), "gelu_tanh": (-40, -37, -28, -20),
        "gelu_t": (-39, -30, -27, -17), "norm_1": (-34, -25, -22, -11),
        "split": (-33, -29, -26, -16, -14, -12, -6, -2, 2.01, 3.02, 8.01), "qk_square": (-31, -24, -18, -10),
        "scores": (-21, -15, -8, 2.02), "probs": (-19, -13, -4, 3.03), "tokens_t": (-9, -7, 16.01, 19.01),
        "logits_copy": (-5, -3, 16.02, 19.03), "top_ratio": (-1, 0.01, 19.02, 25.01),
        "weights_t": (3.01, 7.01, 27.01, 31.01), "combine": (37.01, 43.01),
    },
    "gpsimd": {
        "eps_0": (-73, -71, -69, -68), "rsqrt_0": (-72, -70, -67, -66), "eps_1": (-65, -60, -58, -45),
        "rsqrt_1": (-64, -59, -57, -44), "split": (-63, -53, -50, -47, -46, -43, -28, -17, -16, -12, -3),
        "head_mean": (-62, -56, -49, -33), "head_rsqrt": (-61, -55, -48, -31), "cross_bias": (-54, -52, -51, -18),
        "eps_2": (-42, -40, -8, -2), "rsqrt_2": (-41, -38, -7, -1), "rms_square": (-39, -36, -6, 1.01),
        "rms_eps": (-37, -34, -5, 3.01), "rms_rsqrt": (-35, -32, -4, 3.02), "tokens_lo": (-30, -29, 3.03, 7.02),
        "top_id_float": (-27, -15, 7.03, 16.01), "top_denominator": (-26, -24, 7.01, 12.01),
        "top_first": (-25, -23, 8.01, 12.02), "top_second": (-22, -13, 9.01, 14.01),
        "first_weights": (-21, -14, 10.01, 18.01), "second_weights": (-20, -11, 10.02, 17.01),
        "both_weights": (-19, -10, 10.03, 19.01), "ffn_residual": (-9, 18.02, 27.01, 42.01),
    },
    "sync": {
        "values_copy": (0, 2, 3, 10), "split": (1, 4, 6, 7, 8, 9, 11, 12, 15, 20, 21), "load_w3": (5,),
        "weights_copy": (13, 14, 16, 17), "store": (18, 19),
    },
}
RING = 4
H_RING = 4
DVE_WEIGHTS_FROM = 12
SPLIT = 2


def expert_layout(E, DE):
    pure = DE // P
    main = DE - pure * P
    per_guest = main // (P - main)
    mixed = E * DE // P - E * pure
    assert mixed + mixed // per_guest == E
    return pure, mixed, main, per_guest


def bass_perceiver_block(nc, x, ctx_rows, ctx_cols, wqkv, bqkv, head_w, wo, bo, gate_w, rms_w, w12_d, w3,
                         ident, score_bias, batch_head_mask, value_mask, expert_ids, out):
    N, D = x.shape
    NB, S = ctx_cols.shape[1], ctx_cols.shape[2]
    T = N // NB
    BT = P // T
    NT = N // P
    SC = S // P
    NKV = value_mask.shape[1]
    KV = wqkv.shape[1] - D >> 1
    HD = KV // NKV
    QK = D + KV
    E = gate_w.shape[1]
    CHUNKS = w12_d.shape[2] // P
    DE = w12_d.shape[2] // E
    HALF = 2 * P
    TPH = HALF // P
    HALVES = N // HALF
    STEPS = HALVES * CHUNKS
    YW = KV + NKV
    PURE, MIXED, MAIN, PER_GUEST = expert_layout(E, DE)

    def plan(engine):
        work = [(slot, stage, n) for stage, slots in TIMETABLE[engine].items() for n, slot in enumerate(slots)]
        if engine != "sync":
            work += [(i, "expert", i) for i in range(STEPS)]
        return [(stage, n) for _, stage, n in sorted(work)]

    BANKS = [
        {"cross_scores": "act_done", "scores": "pre_done"},
        {"gelu_t": "actT_done", "probs": "probsT_done"},
        {"latents_t": "xnT0_done", "norm_1": "xnT1_done", "tokens_t": "yT_hi_done"},
        {"cross_out": "x1_done", "qkv": "qk_done", "values": "y_heads_done", "project": "x2_done",
         "route": "logits_copied", "weights_t": "wT_done", "out_t": "out_ready"},
    ]
    FREED_BY = {}
    for bank in BANKS:
        users = [(stage, q) for stage, q in plan("tensor") if stage in bank]
        for (before, q0), user in zip(users, users[1:]):
            FREED_BY[user] = bank[before], q0 + 1

    with ExitStack() as stack:
        def sb(name, shape, dt=F32):
            return stack.enter_context(nc.sbuf_tensor(name, shape, dt))

        def pb(name):
            return stack.enter_context(nc.psum_tensor(name, [P, 512], F32))

        def sem(name):
            return stack.enter_context(nc.semaphore(name))

        x_sb = sb("x_sb", [P, NT, D])
        ctx_r = sb("ctx_r", [P, NB, SC, D])
        ctx_c = sb("ctx_c", [P, NB, S])
        wqkv_sb = sb("wqkv_sb", [P, QK + KV])
        bqkv_sb = sb("bqkv_sb", [P, QK + KV])
        head_sb = sb("head_sb", [P, QK])
        wo_sb = sb("wo_sb", [P, D])
        bo_sb = sb("bo_sb", [P, D])
        gate_sb = sb("gate_sb", [P, E])
        rms_sb = sb("rms_sb", [P, D])
        w12 = sb("w12", [P, RING, 2, SPLIT * P])
        ffn_v = ctx_c[:, 2 * BT:NB, :].rearrange("p b (k t) -> p (b k) t", t=HALF)
        V_RING = (NB - 2 * BT) * S // HALF
        assert E <= 2 * BT
        w_bcast = ctx_c[:, 0:E, :]
        ctx_slots = ctx_r[:, :, :, :].rearrange("p b c d -> p (b c) d")
        w3_sb = ctx_slots[:, 0:CHUNKS, :]
        w_mixed = ctx_slots[:, CHUNKS:CHUNKS + MIXED * NT, :].rearrange("p (m q) d -> p m (q d)", m=MIXED)
        assert CHUNKS <= 2 * BT * SC and CHUNKS + MIXED * NT <= 3 * BT * SC
        ident_sb = sb("ident_sb", [P, P])
        bias_sb = sb("bias_sb", [P, NKV, T])
        bh_mask = sb("bh_mask", [P, BT * NKV])
        v_mask = sb("v_mask", [P, NKV])
        ids_sb = sb("ids_sb", [P, E])
        w12_hi = sb("w12_hi", [P, 2, CHUNKS * P], F32R)
        w12_lo = sb("w12_lo", [P, 2, CHUNKS * P], F32R)

        stats = sb("stats", [P, 3, NT, 6])
        mean_var = sb("mean_var", [P, 3, NT, 2])
        var_eps = sb("var_eps", [P, 3, NT])
        rstd = sb("rstd", [P, 3, NT])
        minus_half = sb("minus_half", [P, D // HD + NKV])
        minus_one = sb("minus_one", [P, 1])
        xn = sb("xn", [P, 3, NT, D])
        xnT = sb("xnT", [P, 3, NT, P])
        gelu_rows = sb("gelu_rows", [P, 2, S])
        actT = sb("actT", [P, 2, SC, P])
        x1 = sb("x1", [P, NT, D])
        qk = sb("qk", [P, NT, QK + KV])
        qk_sq = sb("qk_sq", [P, 2, QK])
        qk_ms = sb("qk_ms", [P, NT, QK // HD])
        qk_rs = sb("qk_rs", [P, NT, QK // HD])
        v_rep = sb("v_rep", [P, NT, BT, KV])
        v_all = sb("v_all", [P, NT, BT, YW])
        qkT = sb("qkT", [P, NT, QK])
        k_blocks = sb("k_blocks", [P, 2, BT * NKV, T])
        pre = sb("pre", [P, 2, BT * NKV, T])
        row_max = sb("row_max", [P, NT, BT * NKV])
        probs = sb("probs", [P, 2, BT * NKV, T])
        probsT = sb("probsT", [P, 2, BT, P])
        inv_sum = sb("inv_sum", [P, NT, BT, NKV])
        y_heads = sb("y_heads", [P, NT, BT, KV])
        yT_heads = sb("yT_heads", [P, NT, P])
        x1b = sb("x1b", [P, NT, D])
        x2 = sb("x2", [P, NT, D])
        rms = sb("rms", [P, NT, 3])
        y_tok = sb("y_tok", [P, NT, D])
        yT = sb("yT", [P, N])
        yT_hi = sb("yT_hi", [P, N], F32R)
        yT_lo = sb("yT_lo", [P, N], F32R)
        resid = sb("resid", [P, NT, D])
        top = sb("top", [P, NT, 8])
        top_id = sb("top_id", [P, NT, 8], U32)
        top_idf = sb("top_idf", [P, NT, 2])
        pick = sb("pick", [P, 5, NT])
        diff, ratio, denom, p_first, p_second = (pick[:, k, :] for k in range(5))
        w_first = sb("w_first", [P, NT, E])
        w_second = sb("w_second", [P, NT, E])
        w_full = sb("w_full", [P, NT, E])
        wT = sb("wT", [E, NT, P])
        logit_sb = sb("logit_sb", [P, NT, E])
        ffn_t = sb("ffn_t", [P, 2, HALF])
        ffn_u = sb("ffn_u", [P, 2, HALF])
        ffn_h = sb("ffn_h", [P, H_RING, HALF])
        combT = sb("combT", [P, HALVES, HALF])

        row_ps = pb("row_ps")
        wide_ps = pb("wide_ps")
        small_ps = pb("small_ps")
        outs_ps = pb("outs_ps")
        expert_ps = [pb(f"expert_ps{i}") for i in range(3)]
        comb_ps = pb("comb_ps")

        names = """x_in consts_in attn_in ffn_small_in w3_in
            powers_set
            stats0_done stats1_done stats2_done mean0_done mean1_done mean2_done var0_done var1_done var2_done
            rstd0_done rstd1_done rstd2_done xn0_done xn1_done xn2_done xnT0_ps xnT1_ps xnT0_done xnT1_done
            h_done sq_done cubic_done th_done act_done actT_ps actT_done cross_done x1_done
            x1b_done head_w_done sums_set qkv_done qk_done qk_sq_done qk_sum_done qk_ms_done qk_rs_done
            v_done qk_scaled qk_ready qkT_done k_blocks_done s_done pre_done max_done centred_done
            probs_done probsT_ps probsT_done y_done inv_done y_heads_done yT_heads_done o_done x2_done
            rms_square_done rms_eps_done rms_done y_tok_done resid_done yT_ps yT_done yT_hi_done yT_lo_done
            logits_done logits_copied top_done top_id_done top_idf_done diff_done exp_done denom_done
            p1_done p2_done w_first_done w_second_done w_full_done wT_ps wT_done w_stored v_stored
            w_hi_done w_lo_done gates_ps tanh_done u_done expert_read weighted_by_gpsimd weighted_by_vector down_done
            combT_done out_ps out_ready stored""".split()
        s = {n: sem(n) for n in names}
        v_rep_in = [sem(f"v_rep_in{q}") for q in range(NT)]
        w_mixed_in = [sem(f"w_mixed_in{q}") for q in range(NT)]
        w_bcast_in = [sem(f"w_bcast_in{q}") for q in range(NT)]
        w12_in = [sem(f"w12_in{n}") for n in range(RING)]
        ctx_in = [sem(f"ctx_in{q}") for q in range(NT)]
        v_dram = nc.dram_tensor("v_dram", (NT, BT, T, KV), F32, kind="Internal").ap()
        w_dram = nc.dram_tensor("w_dram", (NT, E, P), F32, kind="Internal").ap()
        block = stack.enter_context(nc.Block())

        def batches(q):
            return slice(BT * q, BT * q + BT)

        def tile(q):
            return slice(P * q, P * q + P)

        def half(h):
            return slice(HALF * h, HALF * h + HALF)

        def by_vector(i):
            return i >= DVE_WEIGHTS_FROM and i % 2 == 1

        DVE_STEPS = [i for i in range(STEPS) if by_vector(i)]

        def wait_weighted(engine, i):
            count = sum(by_vector(j) == by_vector(i) for j in range(i + 1))
            engine.wait_ge(s["weighted_by_vector" if by_vector(i) else "weighted_by_gpsimd"], count)

        def weights_of(c):
            return w_bcast[:, c // PURE, :] if c < E * PURE else w_mixed[:, c - E * PURE, :]

        def wait_weights(engine, h, c):
            for t in range(TPH * h, TPH * (h + 1)):
                if c < E * PURE:
                    engine.wait_ge(w_bcast_in[t], 16)
                else:
                    engine.wait_ge(w_mixed_in[t], 16 * (1 + E - MIXED))

        @block.sync
        def _(sp):
            def load_w12(n):
                sp.dma_start(w12[:, n % RING, :, :], w12_d[:, :, n * SPLIT * P:(n + 1) * SPLIT * P]).then_inc(w12_in[n % RING], 16)

            sp.dma_start(x_sb[:], x.rearrange("(q p) d -> p q d", p=P)).then_inc(s["x_in"], 16)
            sp.dma_start(ident_sb[:], ident).then_inc(s["consts_in"], 16)
            for q in range(NT):
                if q == NT - 1:
                    for n in range(RING):
                        load_w12(n)
                sp.dma_start(ctx_c[:, batches(q), :], ctx_cols[:, batches(q), :]).then_inc(ctx_in[q], 16)
                sp.dma_start(ctx_r[:, batches(q), :, :], ctx_rows[:, batches(q), :, :]).then_inc(ctx_in[q], 16)
                if q == 0:
                    sp.dma_start(wqkv_sb[:], wqkv).then_inc(s["attn_in"], 16)
                    sp.dma_start(bqkv_sb[:], bqkv.partition_broadcast(P)).then_inc(s["attn_in"], 16)
                    sp.dma_start(head_sb[:], head_w.partition_broadcast(P)).then_inc(s["attn_in"], 16)
                    sp.dma_start(wo_sb[:], wo).then_inc(s["attn_in"], 16)
                    sp.dma_start(bo_sb[:], bo.partition_broadcast(P)).then_inc(s["attn_in"], 16)
                    sp.dma_start(bias_sb[:], score_bias).then_inc(s["attn_in"], 16)
                    sp.dma_start(bh_mask[:], batch_head_mask).then_inc(s["attn_in"], 16)
                    sp.dma_start(v_mask[:], value_mask).then_inc(s["attn_in"], 16)
                    sp.dma_start(gate_sb[:], gate_w).then_inc(s["ffn_small_in"], 16)
                    sp.dma_start(rms_sb[:], rms_w.partition_broadcast(P)).then_inc(s["ffn_small_in"], 16)
                    sp.dma_start(ids_sb[:], expert_ids.partition_broadcast(P)).then_inc(s["ffn_small_in"], 16)
            out_v = out.rearrange("(h t p) d -> h p t d", t=TPH, p=P)
            for stage, q in plan("sync"):
                if stage == "values_copy":
                    sp.wait_ge(s["qk_done"], q + 1)
                    sp.dma_start(v_dram[q].rearrange("b t v -> (b t) v"), qk[:, q, QK:QK + KV]).then_inc(s["v_stored"], 16)
                    sp.wait_ge(s["v_stored"], 16 * (q + 1))
                    for g in range(NKV):
                        sp.dma_start(v_rep[T * g:T * g + T, q, :, :],
                                     v_dram[q].rearrange("b t v -> t b v")).then_inc(v_rep_in[q], 16)
                elif stage == "load_w3":
                    sp.wait_ge(s["cross_done"], 2)
                    sp.dma_start(w3_sb, w3).then_inc(s["w3_in"], 16)
                elif stage == "split" and q + RING < CHUNKS // SPLIT:
                    sp.wait_ge(s["w_lo_done"], q + 1)
                    load_w12(q + RING)
                elif stage == "weights_copy":
                    sp.wait_ge(s["wT_done"], q + 1)
                    sp.dma_start(w_dram[q], wT[:, q, :]).then_inc(s["w_stored"], 16)
                    sp.wait_ge(s["w_stored"], 16 * (q + 1))
                    sp.wait_ge(s["h_done"], 2)
                    sp.dma_start(w_bcast[:, :, tile(q)], w_dram[q].partition_broadcast(P)).then_inc(w_bcast_in[q], 16)
                    sp.wait_ge(s["cross_done"], 3)
                    sp.dma_start(w_mixed[0:MAIN, :, tile(q)],
                                 w_dram[q, 0:MIXED, :].partition_broadcast(MAIN)).then_inc(w_mixed_in[q], 16)
                    for e in range(MIXED, E):
                        n = slice((e - MIXED) * PER_GUEST, (e - MIXED + 1) * PER_GUEST)
                        guests = w_dram[q, e:e + 1, :].broadcast_to([PER_GUEST, P]).partition_broadcast(P - MAIN)
                        sp.dma_start(w_mixed[MAIN:P, n, tile(q)], guests).then_inc(w_mixed_in[q], 16)
                elif stage == "store":
                    sp.wait_ge(s["out_ready"], q + 1)
                    sp.dma_start(out_v[q], resid[:, TPH * q:TPH * (q + 1), :]).then_inc(s["stored"], 16)
            sp.wait_ge(s["stored"], 16 * HALVES)

        ATTN_IN, FFN_SMALL_IN = 16 * 8, 16 * 3

        @block.tensor
        def _(pe):
            pe.wait_ge(s["consts_in"], 16)

            def bank_free(stage, q):
                if (stage, q) in FREED_BY:
                    signal, count = FREED_BY[stage, q]
                    pe.wait_ge(s[signal], count)

            def transpose_rows(q, src, src_ready, done, stage):
                pe.wait_ge(src_ready, q + 1)
                bank_free(stage, q)
                pe.transpose(small_ps[:, 0:P], src, ident_sb[:]).then_inc(done, 1)

            for stage, q in plan("tensor"):
                if stage == "latents_t":
                    transpose_rows(q, xn[:, 0, q, :], s["xn0_done"], s["xnT0_ps"], stage)
                elif stage == "cross_scores":
                    pe.wait_ge(s["xnT0_done"], q + 1)
                    pe.wait_ge(ctx_in[q], 32)
                    bank_free(stage, q)
                    for j in range(BT):
                        mm = pe.matmul(row_ps[T * j:T * j + T, 0:S], xnT[:, 0, q, T * j:T * j + T],
                                       ctx_c[:, BT * q + j, :], start=True, stop=True)
                    mm.then_inc(s["h_done"], 1)
                elif stage == "gelu_t":
                    pe.wait_ge(s["act_done"], q + 1)
                    bank_free(stage, q)
                    for c in range(SC):
                        mm = pe.transpose(wide_ps[:, c * P:c * P + P], gelu_rows[:, q % 2, c * P:c * P + P], ident_sb[:])
                    mm.then_inc(s["actT_ps"], 1)
                elif stage == "cross_out":
                    pe.wait_ge(s["actT_done"], q + 1)
                    bank_free(stage, q)
                    for c in range(SC):
                        for j in range(BT):
                            mm = pe.matmul(outs_ps[T * j:T * j + T, 0:D], actT[:, q % 2, c, T * j:T * j + T],
                                           ctx_r[:, BT * q + j, c, :], start=(c == 0), stop=(c == SC - 1),
                                           skip_group_check=True)
                    mm.then_inc(s["cross_done"], 1)
                elif stage == "norm_1":
                    transpose_rows(q, xn[:, 1, q, :], s["xn1_done"], s["xnT1_ps"], stage)
                elif stage == "qkv":
                    pe.wait_ge(s["xnT1_done"], q + 1)
                    pe.wait_ge(s["attn_in"], ATTN_IN)
                    bank_free(stage, q)
                    pe.matmul(outs_ps[:, 0:QK + KV], xnT[:, 1, q, :], wqkv_sb[:], start=True,
                              stop=True).then_inc(s["qkv_done"], 1)
                elif stage == "scores":
                    pe.wait_ge(s["k_blocks_done"], q + 1)
                    bank_free(stage, q)
                    pe.matmul(row_ps[:, :], qkT[:, q, 0:D], k_blocks[:, q % 2, :, :].rearrange("p a t -> p (a t)"),
                              start=True, stop=True).then_inc(s["s_done"], 1)
                elif stage == "probs":
                    pe.wait_ge(s["probs_done"], q + 1)
                    bank_free(stage, q)
                    for j in range(BT):
                        rows = probs[:, q % 2, NKV * j:NKV * j + NKV, :].rearrange("p a t -> p (a t)")
                        mm = pe.transpose(wide_ps[:, P * j:P * j + P], rows, ident_sb[:])
                    mm.then_inc(s["probsT_ps"], 1)
                elif stage == "values":
                    pe.wait_ge(s["probsT_done"], q + 1)
                    pe.wait_ge(s["v_done"], q + 1)
                    bank_free(stage, q)
                    for j in range(BT):
                        mm = pe.matmul(outs_ps[:, YW * j:YW * j + YW], probsT[:, q % 2, j, :], v_all[:, q, j, :],
                                       start=True, stop=True)
                    mm.then_inc(s["y_done"], 1)
                elif stage == "project":
                    pe.wait_ge(s["yT_heads_done"], q + 1)
                    bank_free(stage, q)
                    pe.matmul(outs_ps[:, 0:D], yT_heads[:, q, :], wo_sb[:], start=True, stop=True).then_inc(s["o_done"], 1)
                elif stage == "tokens_t":
                    transpose_rows(q, y_tok[:, q, :], s["y_tok_done"], s["yT_ps"], stage)
                elif stage == "route":
                    pe.wait_ge(s["yT_done"], q + 1)
                    pe.wait_ge(s["ffn_small_in"], FFN_SMALL_IN)
                    bank_free(stage, q)
                    pe.matmul(outs_ps[:, 0:E], yT[:, tile(q)], gate_sb[:], start=True, stop=True).then_inc(s["logits_done"], 1)
                elif stage == "weights_t":
                    pe.wait_ge(s["w_full_done"], q + 1)
                    bank_free(stage, q)
                    pe.transpose(outs_ps[0:E, 0:P], w_full[:, q, :], ident_sb[:]).then_inc(s["wT_ps"], 1)
                elif stage == "expert":
                    i = q
                    h, c = divmod(i, CHUNKS)
                    if c == 0:
                        pe.wait_ge(s["yT_hi_done"], TPH * (h + 1))
                        pe.wait_ge(s["yT_lo_done"], TPH * (h + 1))
                    if h == 0:
                        pe.wait_ge(s["w_lo_done"], c // SPLIT + 1)
                    if i >= 3:
                        pe.wait_ge(s["expert_read"], i - 2)
                    cols = slice(c * P, c * P + P)
                    for k in range(2):
                        o = expert_ps[i % 3][:, HALF * k:HALF * k + HALF]
                        pe.matmul(o, w12_hi[:, k, cols], yT_hi[:, half(h)], start=True, stop=False)
                        pe.matmul(o, w12_hi[:, k, cols], yT_lo[:, half(h)], start=False, stop=False)
                        mm = pe.matmul(o, w12_lo[:, k, cols], yT_hi[:, half(h)], start=False, stop=True)
                    mm.then_inc(s["gates_ps"], 1)
                elif stage == "down":
                    i = q
                    h, c = divmod(i, CHUNKS)
                    wait_weighted(pe, i)
                    if i == 0:
                        pe.wait_ge(s["w3_in"], 16)
                    if c == 0 and h:
                        pe.wait_ge(s["combT_done"], h)
                    pe.matmul(comb_ps[:, 0:HALF], w3_sb[:, c, :], ffn_h[:, i % H_RING, :],
                              start=(c == 0), stop=(c == CHUNKS - 1)).then_inc(s["down_done"], 1)
                elif stage == "out_t":
                    pe.wait_ge(s["combT_done"], q + 1)
                    bank_free(stage, q)
                    for t in range(TPH):
                        mm = pe.transpose(outs_ps[:, P * t:P * t + P], combT[:, q, P * t:P * t + P], ident_sb[:])
                    mm.then_inc(s["out_ps"], 1)

        @block.scalar
        def _(act):
            for stage, q in plan("scalar"):
                if stage == "latents_t":
                    act.wait_ge(s["xnT0_ps"], q + 1)
                    act.activation(xnT[:, 0, q, :], small_ps[:, 0:P], ACT.Copy).then_inc(s["xnT0_done"], 1)
                elif stage == "gelu_square":
                    act.wait_ge(s["h_done"], q + 1)
                    if q >= 2:
                        act.wait_ge(s["actT_ps"], q - 1)
                    act.activation(gelu_rows[:, q % 2, :], row_ps[:, :], ACT.Square).then_inc(s["sq_done"], 1)
                elif stage == "gelu_tanh":
                    act.wait_ge(s["cubic_done"], q + 1)
                    act.activation(gelu_rows[:, q % 2, :], gelu_rows[:, q % 2, :], ACT.Tanh,
                                   scale=GELU_SCALE * GELU_CUBIC).then_inc(s["th_done"], 1)
                elif stage == "gelu_t":
                    act.wait_ge(s["actT_ps"], q + 1)
                    if q >= 2:
                        act.wait_ge(s["cross_done"], q - 1)
                    act.activation(actT[:, q % 2, :, :].rearrange("p c t -> p (c t)"), wide_ps[:, :],
                                   ACT.Copy).then_inc(s["actT_done"], 1)
                elif stage == "norm_1":
                    act.wait_ge(s["xnT1_ps"], q + 1)
                    act.activation(xnT[:, 1, q, :], small_ps[:, 0:P], ACT.Copy).then_inc(s["xnT1_done"], 1)
                elif stage == "scores":
                    act.wait_ge(s["centred_done"], q + 1)
                    if q >= 2:
                        act.wait_ge(s["probsT_ps"], q - 1)
                    act.activation(probs[:, q % 2, :, :], pre[:, q % 2, :, :], ACT.Exp).then_inc(s["probs_done"], 1)
                elif stage == "probs":
                    act.wait_ge(s["probsT_ps"], q + 1)
                    if q >= 2:
                        act.wait_ge(s["y_done"], q - 1)
                    act.activation(probsT[:, q % 2, :, :].rearrange("p c t -> p (c t)"), wide_ps[:, :],
                                   ACT.Copy).then_inc(s["probsT_done"], 1)
                elif stage == "tokens_t":
                    act.wait_ge(s["yT_ps"], q + 1)
                    act.activation(yT[:, tile(q)], small_ps[:, 0:P], ACT.Copy).then_inc(s["yT_done"], 1)
                    act.activation(yT_hi[:, tile(q)], small_ps[:, 0:P], ACT.Copy).then_inc(s["yT_hi_done"], 1)
                elif stage == "qk_square":
                    act.wait_ge(s["qk_done"], q + 1)
                    if q >= 2:
                        act.wait_ge(s["qk_sum_done"], q - 1)
                    act.activation(qk_sq[:, q % 2, :], qk[:, q, 0:QK], ACT.Square).then_inc(s["qk_sq_done"], 1)
                elif stage == "logits_copy":
                    act.wait_ge(s["logits_done"], q + 1)
                    act.activation(logit_sb[:, q, :], outs_ps[:, 0:E], ACT.Copy).then_inc(s["logits_copied"], 1)
                elif stage == "weights_t":
                    act.wait_ge(s["wT_ps"], q + 1)
                    act.activation(wT[:, q, :], outs_ps[0:E, 0:P], ACT.Copy).then_inc(s["wT_done"], 1)
                elif stage == "top_ratio":
                    act.wait_ge(s["diff_done"], q + 1)
                    act.activation(ratio[:, q:q + 1], diff[:, q:q + 1], ACT.Exp).then_inc(s["exp_done"], 1)
                elif stage == "split":
                    cols = slice(q * SPLIT * P, (q + 1) * SPLIT * P)
                    act.wait_ge(w12_in[q % RING], 16 * (q // RING + 1))
                    act.activation(w12_hi[:, :, cols], w12[:, q % RING, :, :], ACT.Copy).then_inc(s["w_hi_done"], 1)
                elif stage == "expert":
                    i = q
                    act.wait_ge(s["gates_ps"], i + 1)
                    if i >= 2:
                        act.wait_ge(s["u_done"], i - 1)
                    act.activation(ffn_t[:, i % 2, :], expert_ps[i % 3][:, 0:HALF], ACT.Tanh,
                                   scale=0.5).then_inc(s["tanh_done"], 1)
                elif stage == "combine":
                    act.wait_ge(s["down_done"], CHUNKS * (q + 1))
                    act.activation(combT[:, q, :], comb_ps[:, 0:HALF], ACT.Copy, scale=0.5).then_inc(s["combT_done"], 1)

        @block.gpsimd
        def _(pool):
            pool.memset(minus_half[:], -0.5).then_inc(s["powers_set"], 1)
            pool.memset(minus_one[:], -1.0).then_inc(s["powers_set"], 1)
            pool.wait_ge(s["powers_set"], 2)

            def add_eps(k, q):
                pool.wait_ge(s[f"mean{k}_done"], q + 1)
                pool.tensor_scalar(var_eps[:, k, q:q + 1], mean_var[:, k, q, 1:2], LN_EPS, None,
                                   ALU.add).then_inc(s[f"var{k}_done"], 1)

            def rsqrt(k, q):
                pool.wait_ge(s[f"var{k}_done"], q + 1)
                pool.tensor_tensor(rstd[:, k, q:q + 1], var_eps[:, k, q:q + 1], minus_half[:, 0:1],
                                   ALU.pow).then_inc(s[f"rstd{k}_done"], 1)

            for stage, q in plan("gpsimd"):
                if stage.startswith("eps_"):
                    add_eps(int(stage[-1]), q)
                elif stage.startswith("rsqrt_"):
                    rsqrt(int(stage[-1]), q)
                elif stage == "cross_bias":
                    pool.wait_ge(s["x1_done"], q + 1)
                    pool.wait_ge(s["attn_in"], ATTN_IN)
                    pool.tensor_tensor(x1b[:, q, :], x1[:, q, :], bo_sb[:], ALU.add).then_inc(s["x1b_done"], 1)
                elif stage == "head_mean":
                    pool.wait_ge(s["qk_sum_done"], q + 1)
                    pool.tensor_scalar(qk_ms[:, q, :], qk_ms[:, q, :], 1.0 / HD, QK_EPS, ALU.mult,
                                       ALU.add).then_inc(s["qk_ms_done"], 1)
                elif stage == "head_rsqrt":
                    pool.wait_ge(s["qk_ms_done"], q + 1)
                    pool.tensor_tensor(qk_rs[:, q, :], qk_ms[:, q, :], minus_half[:, 0:QK // HD],
                                       ALU.pow).then_inc(s["qk_rs_done"], 1)
                elif stage.startswith("rms_"):
                    r, v, m = rstd[:, 2, q:q + 1], mean_var[:, 2, q, 1:2], [rms[:, q, k:k + 1] for k in range(3)]
                    if stage == "rms_square":
                        pool.wait_ge(s["rstd2_done"], q + 1)
                        pool.tensor_tensor(m[0], r, r, ALU.mult).then_inc(s["rms_square_done"], 1)
                    elif stage == "rms_eps":
                        pool.wait_ge(s["rms_square_done"], q + 1)
                        pool.tensor_scalar(m[1], m[0], v, RMS_EPS, ALU.mult, ALU.add).then_inc(s["rms_eps_done"], 1)
                    elif stage == "rms_rsqrt":
                        pool.wait_ge(s["rms_eps_done"], q + 1)
                        pool.tensor_tensor(m[2], m[1], minus_half[:, 0:1], ALU.pow).then_inc(s["rms_done"], 1)
                elif stage == "ffn_residual":
                    pool.wait_ge(s["xn2_done"], q + 1)
                    pool.tensor_tensor(resid[:, q, :], x2[:, q, :], xn[:, 2, q, :], ALU.add).then_inc(s["resid_done"], 1)
                elif stage == "top_id_float":
                    pool.wait_ge(s["top_id_done"], q + 1)
                    pool.tensor_copy(top_idf[:, q, :], top_id[:, q, 0:2]).then_inc(s["top_idf_done"], 1)
                elif stage == "top_denominator":
                    pool.wait_ge(s["exp_done"], q + 1)
                    pool.tensor_scalar(denom[:, q:q + 1], ratio[:, q:q + 1], 1.0, None, ALU.add).then_inc(s["denom_done"], 1)
                elif stage == "top_first":
                    pool.wait_ge(s["denom_done"], q + 1)
                    pool.tensor_tensor(p_first[:, q:q + 1], denom[:, q:q + 1], minus_one[:, 0:1],
                                       ALU.pow).then_inc(s["p1_done"], 1)
                elif stage == "top_second":
                    pool.wait_ge(s["p1_done"], q + 1)
                    pool.tensor_tensor(p_second[:, q:q + 1], ratio[:, q:q + 1], p_first[:, q:q + 1],
                                       ALU.mult).then_inc(s["p2_done"], 1)
                elif stage == "first_weights":
                    pool.wait_ge(s["ffn_small_in"], FFN_SMALL_IN)
                    pool.wait_ge(s["p1_done"], q + 1)
                    pool.wait_ge(s["top_idf_done"], q + 1)
                    pool.tensor_scalar(w_first[:, q, :], ids_sb[:], top_idf[:, q, 0:1], p_first[:, q:q + 1],
                                       ALU.is_equal, ALU.mult).then_inc(s["w_first_done"], 1)
                elif stage == "second_weights":
                    pool.wait_ge(s["ffn_small_in"], FFN_SMALL_IN)
                    pool.wait_ge(s["p2_done"], q + 1)
                    pool.wait_ge(s["top_idf_done"], q + 1)
                    pool.tensor_scalar(w_second[:, q, :], ids_sb[:], top_idf[:, q, 1:2], p_second[:, q:q + 1],
                                       ALU.is_equal, ALU.mult).then_inc(s["w_second_done"], 1)
                elif stage == "both_weights":
                    pool.wait_ge(s["w_first_done"], q + 1)
                    pool.wait_ge(s["w_second_done"], q + 1)
                    pool.tensor_tensor(w_full[:, q, :], w_first[:, q, :], w_second[:, q, :], ALU.add).then_inc(s["w_full_done"], 1)
                elif stage == "split":
                    cols = slice(q * SPLIT * P, (q + 1) * SPLIT * P)
                    pool.wait_ge(s["w_hi_done"], q + 1)
                    pool.tensor_tensor(w12_lo[:, :, cols], w12[:, q % RING, :, :], w12_hi[:, :, cols].bitcast(F32),
                                       ALU.subtract).then_inc(s["w_lo_done"], 1)
                elif stage == "tokens_lo":
                    pool.wait_ge(s["yT_done"], q + 1)
                    pool.wait_ge(s["yT_hi_done"], q + 1)
                    pool.tensor_tensor(yT_lo[:, tile(q)], yT[:, tile(q)], yT_hi[:, tile(q)].bitcast(F32),
                                       ALU.subtract).then_inc(s["yT_lo_done"], 1)
                elif stage == "expert":
                    i = q
                    if by_vector(i):
                        continue
                    h, c = divmod(i, CHUNKS)
                    pool.wait_ge(s["expert_read"], i + 1)
                    wait_weights(pool, h, c)
                    if i >= H_RING:
                        pool.wait_ge(s["down_done"], i - H_RING + 1)
                    pool.tensor_tensor(ffn_h[:, i % H_RING, :], ffn_v[:, i % V_RING, :], weights_of(c)[:, half(h)],
                                       ALU.mult).then_inc(s["weighted_by_gpsimd"], 1)

        @block.vector
        def _(dve):
            def row_stats(k, q, src):
                dve.bn_stats(stats[:, k, q, :], src).then_inc(s[f"stats{k}_done"], 1)

            def row_mean(k, q):
                dve.wait_ge(s[f"stats{k}_done"], q + 1)
                dve.bn_aggr(mean_var[:, k, q, :], stats[:, k, q, :]).then_inc(s[f"mean{k}_done"], 1)

            def normalise(k, q, src):
                dve.wait_ge(s[f"rstd{k}_done"], q + 1)
                dve.tensor_scalar(xn[:, k, q, :], src, mean_var[:, k, q, 0:1], rstd[:, k, q:q + 1],
                                  ALU.subtract, ALU.mult).then_inc(s[f"xn{k}_done"], 1)

            attn_ps = outs_ps[:, 0:BT * YW].rearrange("p (b n) -> p b n", n=YW)
            dve.wait_ge(s["x_in"], 16)
            for stage, q in plan("vector"):
                if stage == "stats_0":
                    row_stats(0, q, x_sb[:, q, :])
                elif stage == "mean_0":
                    row_mean(0, q)
                elif stage == "norm_0":
                    normalise(0, q, x_sb[:, q, :])
                elif stage == "gelu_cubic":
                    dve.wait_ge(s["sq_done"], q + 1)
                    dve.scalar_tensor_tensor(out=gelu_rows[:, q % 2, :], in0=gelu_rows[:, q % 2, :], scalar=1.0 / GELU_CUBIC,
                                             in1=row_ps[:, :], op0=ALU.add, op1=ALU.mult).then_inc(s["cubic_done"], 1)
                elif stage == "gelu":
                    dve.wait_ge(s["th_done"], q + 1)
                    dve.scalar_tensor_tensor(out=gelu_rows[:, q % 2, :], in0=gelu_rows[:, q % 2, :], scalar=1.0,
                                             in1=row_ps[:, :], op0=ALU.add,
                                             op1=ALU.mult).then_inc(s["act_done"], 1)
                elif stage == "cross_residual":
                    dve.wait_ge(s["cross_done"], q + 1)
                    dve.scalar_tensor_tensor(out=x1[:, q, :], in0=outs_ps[:, 0:D], scalar=0.5, in1=x_sb[:, q, :],
                                             op0=ALU.mult, op1=ALU.add).then_inc(s["x1_done"], 1)
                elif stage == "stats_1":
                    dve.wait_ge(s["x1_done"], q + 1)
                    row_stats(1, q, x1[:, q, :])
                elif stage == "mean_1":
                    row_mean(1, q)
                elif stage == "norm_1":
                    normalise(1, q, x1[:, q, :])
                elif stage == "attn_constants":
                    dve.wait_ge(s["attn_in"], ATTN_IN)
                    dve.tensor_scalar(head_sb[:, 0:D], head_sb[:, 0:D], float(HD) ** -0.5, None,
                                      ALU.mult).then_inc(s["head_w_done"], 1)
                    dve.tensor_copy(v_all[:, :, :, KV:YW].rearrange("p q b g -> p (q b) g"),
                                    v_mask[:].unsqueeze(1).broadcast_to([P, NT * BT, NKV])).then_inc(s["sums_set"], 1)
                elif stage == "qkv_bias":
                    dve.wait_ge(s["attn_in"], ATTN_IN)
                    dve.wait_ge(s["qkv_done"], q + 1)
                    dve.tensor_tensor(qk[:, q, :], outs_ps[:, 0:QK + KV], bqkv_sb[:], ALU.add).then_inc(s["qk_done"], 1)
                elif stage == "qk_sum":
                    dve.wait_ge(s["qk_sq_done"], q + 1)
                    dve.tensor_reduce(qk_ms[:, q, :], qk_sq[:, q % 2, :].rearrange("p (h d) -> p h d", d=HD),
                                      AX_X, ALU.add).then_inc(s["qk_sum_done"], 1)
                elif stage == "head_scale":
                    dve.wait_ge(s["qk_rs_done"], q + 1)
                    heads = qk[:, q, 0:QK].rearrange("p (h d) -> p h d", d=HD)
                    dve.tensor_tensor(heads, heads, qk_rs[:, q, :].unsqueeze(2).broadcast_to([P, QK // HD, HD]),
                                      ALU.mult).then_inc(s["qk_scaled"], 1)
                elif stage == "head_weights":
                    dve.wait_ge(s["qk_scaled"], q + 1)
                    dve.wait_ge(s["head_w_done"], 1)
                    dve.tensor_tensor(qk[:, q, 0:QK], qk[:, q, 0:QK], head_sb[:], ALU.mult).then_inc(s["qk_ready"], 1)
                elif stage == "heads_t":
                    dve.wait_ge(s["qk_ready"], q + 1)
                    dve.transpose(qkT[:, q, :], qk[:, q, 0:QK]).then_inc(s["qkT_done"], 1)
                elif stage == "key_blocks":
                    dve.wait_ge(s["qkT_done"], q + 1)
                    if q >= 2:
                        dve.wait_ge(s["s_done"], q - 1)
                    dve.tensor_tensor(k_blocks[:, q % 2, :, :],
                                      qkT[:, q, D:QK].unsqueeze(1).broadcast_to([P, BT * NKV, T]),
                                      bh_mask[:].unsqueeze(2).broadcast_to([P, BT * NKV, T]),
                                      ALU.mult).then_inc(s["k_blocks_done"], 1)
                elif stage == "score_bias":
                    dve.wait_ge(s["s_done"], q + 1)
                    if q >= 2:
                        dve.wait_ge(s["probs_done"], q - 1)
                    flat = pre[:, q % 2, :, :].rearrange("p (b g) t -> p b (g t)", g=NKV)
                    dve.tensor_tensor(flat, row_ps[:, :].rearrange("p (b n) -> p b n", b=BT),
                                      bias_sb[:].rearrange("p g t -> p (g t)").unsqueeze(1).broadcast_to([P, BT, NKV * T]),
                                      ALU.add).then_inc(s["pre_done"], 1)
                elif stage == "score_max":
                    dve.wait_ge(s["pre_done"], q + 1)
                    dve.tensor_reduce(row_max[:, q, :], pre[:, q % 2, :, :], AX_X, ALU.max).then_inc(s["max_done"], 1)
                elif stage == "score_centre":
                    dve.wait_ge(s["max_done"], q + 1)
                    dve.tensor_tensor(pre[:, q % 2, :, :], pre[:, q % 2, :, :],
                                      row_max[:, q, :].unsqueeze(2).broadcast_to([P, BT * NKV, T]),
                                      ALU.subtract).then_inc(s["centred_done"], 1)
                elif stage == "value_rows":
                    dve.wait_ge(v_rep_in[q], 16 * NKV)
                    dve.wait_ge(s["sums_set"], 1)
                    dve.tensor_tensor(v_all[:, q, :, 0:KV].rearrange("p b (g d) -> p b g d", g=NKV),
                                      v_rep[:, q, :, :].rearrange("p b (g d) -> p b g d", g=NKV),
                                      v_mask[:].unsqueeze(1).unsqueeze(3).broadcast_to([P, BT, NKV, HD]),
                                      ALU.mult).then_inc(s["v_done"], 1)
                elif stage == "sums_inverse":
                    dve.wait_ge(s["y_done"], q + 1)
                    dve.reciprocal(inv_sum[:, q, :, :], attn_ps[:, :, KV:YW]).then_inc(s["inv_done"], 1)
                elif stage == "value_scale":
                    dve.wait_ge(s["inv_done"], q + 1)
                    dve.tensor_tensor(y_heads[:, q, :, :].rearrange("p b (g d) -> p b g d", g=NKV),
                                      attn_ps[:, :, 0:KV].rearrange("p b (g d) -> p b g d", g=NKV),
                                      inv_sum[:, q, :, :].unsqueeze(3).broadcast_to([P, BT, NKV, HD]),
                                      ALU.mult).then_inc(s["y_heads_done"], 1)
                elif stage == "values_t":
                    dve.wait_ge(s["y_heads_done"], q + 1)
                    dve.transpose(yT_heads[:, q, :], y_heads[:, q, :, :].rearrange("p b v -> p (b v)")).then_inc(s["yT_heads_done"], 1)
                elif stage == "attn_residual":
                    dve.wait_ge(s["o_done"], q + 1)
                    dve.wait_ge(s["x1b_done"], q + 1)
                    dve.tensor_tensor(x2[:, q, :], outs_ps[:, 0:D], x1b[:, q, :], ALU.add).then_inc(s["x2_done"], 1)
                elif stage == "stats_2":
                    dve.wait_ge(s["x2_done"], q + 1)
                    row_stats(2, q, x2[:, q, :])
                elif stage == "mean_2":
                    row_mean(2, q)
                elif stage == "norm_2":
                    normalise(2, q, x2[:, q, :])
                elif stage == "token_scale":
                    dve.wait_ge(s["xn2_done"], q + 1)
                    dve.wait_ge(s["rms_done"], q + 1)
                    dve.wait_ge(s["ffn_small_in"], FFN_SMALL_IN)
                    dve.scalar_tensor_tensor(out=y_tok[:, q, :], in0=xn[:, 2, q, :], scalar=rms[:, q, 2:3],
                                             in1=rms_sb[:], op0=ALU.mult, op1=ALU.mult).then_inc(s["y_tok_done"], 1)
                elif stage == "top_two":
                    dve.wait_ge(s["logits_copied"], q + 1)
                    dve.max(top[:, q, :], logit_sb[:, q, :]).then_inc(s["top_done"], 1)
                elif stage == "top_difference":
                    one = slice(q, q + 1)
                    dve.wait_ge(s["top_done"], q + 1)
                    dve.tensor_tensor(diff[:, one], top[:, q, 1:2], top[:, q, 0:1], ALU.subtract).then_inc(s["diff_done"], 1)
                elif stage == "top_index":
                    dve.wait_ge(s["top_done"], q + 1)
                    dve.max_index(top_id[:, q, :], top[:, q, :], logit_sb[:, q, :]).then_inc(s["top_id_done"], 1)
                elif stage == "expert":
                    i = q
                    up, gate = expert_ps[i % 3][:, 0:HALF], expert_ps[i % 3][:, HALF:2 * HALF]
                    dve.wait_ge(s["tanh_done"], i + 1)
                    dve.scalar_tensor_tensor(out=ffn_u[:, i % 2, :], in0=ffn_t[:, i % 2, :], scalar=1.0, in1=up,
                                             op0=ALU.add, op1=ALU.mult).then_inc(s["u_done"], 1)
                    dve.wait_ge(s["u_done"], i + 1)
                    if i == 0:
                        dve.wait_ge(s["h_done"], NT)
                    if i >= V_RING:
                        wait_weighted(dve, i - V_RING)
                    dve.tensor_tensor(ffn_v[:, i % V_RING, :], ffn_u[:, i % 2, :], gate, ALU.mult).then_inc(s["expert_read"], 1)
                elif stage == "weigh":
                    i = DVE_STEPS[q]
                    h, c = divmod(i, CHUNKS)
                    dve.wait_ge(s["expert_read"], i + 1)
                    wait_weights(dve, h, c)
                    dve.wait_ge(s["down_done"], i - H_RING + 1)
                    dve.tensor_tensor(ffn_h[:, i % H_RING, :], ffn_v[:, i % V_RING, :], weights_of(c)[:, half(h)],
                                      ALU.mult).then_inc(s["weighted_by_vector"], 1)
                elif stage == "output":
                    dve.wait_ge(s["out_ps"], q + 1)
                    dve.wait_ge(s["resid_done"], TPH * (q + 1))
                    rows = resid[:, TPH * q:TPH * (q + 1), :].rearrange("p t d -> p (t d)")
                    dve.tensor_tensor(rows, rows, outs_ps[:, 0:HALF], ALU.add).then_inc(s["out_ready"], 1)


def kernel(x, ctx_1024, L0_attn_wq, L0_attn_bq, L0_attn_wkv, L0_attn_bkv, L0_attn_wo, L0_attn_bo,
           L0_attn_qn_w, L0_attn_kn_w, L0_ffn_gate_w, L0_ffn_rms_w, L0_ffn_W1, L0_ffn_W2, L0_ffn_W3):
    import numpy as np
    import concourse.bacc as bacc
    from concourse.bass_utils import run_bass_kernel_spmd

    x, ctx = np.asarray(x), np.asarray(ctx_1024)
    NB, T, D = x.shape
    S = ctx.shape[1]
    HD = L0_attn_qn_w.shape[0]
    H = D // HD
    KV = L0_attn_wkv.shape[1] // 2
    NKV = KV // HD
    REP = H // NKV
    E, DE = L0_ffn_W1.shape[:2]
    BT = P // T
    f32 = np.float32

    def grouped(a):
        a = np.asarray(a)
        return a.reshape(a.shape[:-1] + (NKV, REP, HD)).swapaxes(-3, -2).reshape(a.shape)

    part = np.arange(P)
    slopes = (2.0 ** (-(np.arange(H, dtype=f32) / f32(H - 1) * f32(8.0)))).astype(f32)
    head = np.arange(NKV)[None, :] * REP + (part // T)[:, None]
    dist = ((part % T)[:, None] - np.arange(T)[None, :])[:, None, :]
    score_bias = np.where(dist < 0, f32(-1e30), -slopes[head][:, :, None] * np.abs(dist).astype(f32)).astype(f32)
    batch_head_mask = ((part // HD)[:, None] == np.arange(BT * NKV)[None, :]).astype(f32)
    value_mask = ((part // T)[:, None] == np.arange(NKV)[None, :]).astype(f32)

    pure, mixed, main, per_guest = expert_layout(E, DE)
    feature = np.arange(E * DE).reshape(E, DE)
    guest = P - main
    order = [feature[:, :pure * P].reshape(-1)]
    for n in range(mixed):
        at = pure * P + n % per_guest * guest
        order += [feature[n, pure * P:], feature[mixed + n // per_guest, at:at + guest]]
    order = np.concatenate(order)

    arrays = {
        "x": x.reshape(NB * T, D),
        "ctx_rows": ctx.reshape(NB, S // P, P, D).transpose(2, 0, 1, 3),
        "ctx_cols": ctx.transpose(2, 0, 1),
        "wqkv": np.concatenate([grouped(L0_attn_wq), np.asarray(L0_attn_wkv)], axis=1),
        "bqkv": np.concatenate([grouped(L0_attn_bq), np.asarray(L0_attn_bkv)]),
        "head_w": np.concatenate([np.tile(np.asarray(L0_attn_qn_w), H), np.tile(np.asarray(L0_attn_kn_w), NKV)]),
        "wo": np.ascontiguousarray(grouped(np.asarray(L0_attn_wo).T).T),
        "bo": np.asarray(L0_attn_bo),
        "gate_w": np.asarray(L0_ffn_gate_w).T,
        "rms_w": np.asarray(L0_ffn_rms_w),
        "w12": np.stack([np.asarray(w).reshape(E * DE, D)[order].T for w in (L0_ffn_W1, L0_ffn_W2)], axis=1),
        "w3": np.asarray(L0_ffn_W3).transpose(0, 2, 1).reshape(E * DE, D)[order].reshape(-1, P, D).transpose(1, 0, 2),
        "ident": np.eye(P, dtype=f32),
        "score_bias": score_bias,
        "batch_head_mask": batch_head_mask,
        "value_mask": value_mask,
        "expert_ids": np.arange(E, dtype=f32),
    }
    arrays = {f"in_{n}": np.ascontiguousarray(a) for n, a in arrays.items()}
    nc = bacc.Bacc("TRN2", target_bir_lowering=False, num_devices=1)
    args = [nc.dram_tensor(n, a.shape, F32, kind="ExternalInput").ap() for n, a in arrays.items()]
    args.append(nc.dram_tensor("out_0", (NB * T, D), F32, kind="ExternalOutput").ap())
    bass_perceiver_block(nc, *args)
    r = run_bass_kernel_spmd(nc, [arrays], core_ids=[0])
    return r.results[0]["out_0"].reshape(NB, T, D)
```
